# Optimizing a Trainium2 kernel written in Bass

```python
import numpy as np
import jax
import jax.numpy as jnp

def _softmax(x, axis=-1):
    return jax.nn.softmax(x, axis=axis)

def _gelu(x):
    return jax.nn.gelu(x, approximate=True)

def _silu(x):
    return jax.nn.silu(x)

def _sigmoid(x):
    return jax.nn.sigmoid(x)

def _layernorm(x, axis=-1, eps=1e-05):
    m = jnp.mean(x, axis=axis, keepdims=True)
    v = jnp.var(x, axis=axis, keepdims=True)
    return (x - m) / jnp.sqrt(v + eps)

def _scatter_add(tgt, idx, src, axis=0):
    return tgt.at[idx].add(src)

def _segment_sum(src, seg, n):
    return jax.ops.segment_sum(src, seg, n)
kernel_name = 'mk_adj_resnorm_d1_adj_r2_b901a1'

def setup_inputs(seed: int=0):
    np.random.seed(seed)
    _w = jnp.asarray

    def _rec_inputs():
        import jax
        import jax.numpy as jnp
        _gk = jax.random.key(seed)
        x = -1.394e-06 + 0.9999 * jax.random.normal(jax.random.fold_in(_gk, 1), (4096, 256), jnp.float32)
        _a = jax.random.bernoulli(jax.random.fold_in(_gk, 2), 0.000488281, (4096, 4096))
        _a = jnp.logical_or(_a, jnp.eye(4096, dtype=bool))
        adj = _a
        return (x, adj)
    x, adj = _rec_inputs()

    def _L0_gnn_setup():
        import jax, jax.numpy as jnp
        import numpy as np
        import math
        N = 4096
        D_IN = 256
        LOCAL_D = 256
        GLOBAL_D = 256
        key = jax.random.key(seed)
        ks = jax.random.split(key, 16)
        s = 1.0 / math.sqrt(D_IN)
        adj = jax.random.bernoulli(ks[0], 0.01, (N, N))
        adj = adj | jnp.eye(N, dtype=bool)
        return {'adj_matrix': adj, 'x': jax.random.normal(ks[1], (N, D_IN), jnp.float32), 'masked_x': jax.random.normal(ks[2], (N, D_IN), jnp.float32), 'Wlq': jax.random.normal(ks[3], (D_IN, LOCAL_D), jnp.float32) * s, 'Wlk': jax.random.normal(ks[4], (D_IN, LOCAL_D), jnp.float32) * s, 'Wlv': jax.random.normal(ks[5], (D_IN, D_IN), jnp.float32) * s, 'blv': jax.random.normal(ks[6], (D_IN,), jnp.float32) * 0.01, 'Wgq': jax.random.normal(ks[7], (D_IN, GLOBAL_D), jnp.float32) * s, 'Wgk': jax.random.normal(ks[8], (D_IN, GLOBAL_D), jnp.float32) * s, 'Wgv': jax.random.normal(ks[9], (D_IN, D_IN), jnp.float32) * s, 'bgv': jax.random.normal(ks[10], (D_IN,), jnp.float32) * 0.01, 'Wes': jax.random.normal(ks[11], (D_IN, 1), jnp.float32) * s, 'Wev': jax.random.normal(ks[12], (D_IN, D_IN), jnp.float32) * s, 'bev': jax.random.normal(ks[13], (D_IN,), jnp.float32) * 0.01}
    _L0_gnn_all = _L0_gnn_setup()
    _L0_gnn_in = {k: v for k, v in _L0_gnn_all.items() if k in ('masked_x', 'Wlq', 'Wlk', 'Wlv', 'blv', 'Wgq', 'Wgk', 'Wgv', 'bgv', 'Wes', 'Wev', 'bev')}
    del _L0_gnn_all
    return {'x': x, 'adj': adj, 'L0_gnn_masked_x': _L0_gnn_in['masked_x'], 'L0_gnn_Wlq': _L0_gnn_in['Wlq'], 'L0_gnn_Wlk': _L0_gnn_in['Wlk'], 'L0_gnn_Wlv': _L0_gnn_in['Wlv'], 'L0_gnn_blv': _L0_gnn_in['blv'], 'L0_gnn_Wgq': _L0_gnn_in['Wgq'], 'L0_gnn_Wgk': _L0_gnn_in['Wgk'], 'L0_gnn_Wgv': _L0_gnn_in['Wgv'], 'L0_gnn_bgv': _L0_gnn_in['bgv'], 'L0_gnn_Wes': _L0_gnn_in['Wes'], 'L0_gnn_Wev': _L0_gnn_in['Wev'], 'L0_gnn_bev': _L0_gnn_in['bev']}

def reference(x, adj, L0_gnn_masked_x, L0_gnn_Wlq, L0_gnn_Wlk, L0_gnn_Wlv, L0_gnn_blv, L0_gnn_Wgq, L0_gnn_Wgk, L0_gnn_Wgv, L0_gnn_bgv, L0_gnn_Wes, L0_gnn_Wev, L0_gnn_bev):
    import jax
    import jax.numpy as jnp

    def _L0_gnn_ref(adj_matrix, x, masked_x, Wlq, Wlk, Wlv, blv, Wgq, Wgk, Wgv, bgv, Wes, Wev, bev):
        import jax, jax.numpy as jnp
        import numpy as np
        import math
        N = 4096
        D_IN = 256
        LOCAL_D = 256
        GLOBAL_D = 256
        scale = 1.0 / math.sqrt(D_IN)
        x_bar = jnp.mean(x, axis=0, keepdims=True)
        lQ = masked_x @ Wlq
        lK = x @ Wlk
        lV = x @ Wlv + blv
        gQ = masked_x @ Wgq
        gK = x_bar @ Wgk
        gV = x_bar @ Wgv + bgv
        es = masked_x @ Wes
        eV = masked_x @ Wev + bev
        local_scores = lQ @ lK.T * scale
        local_scores = jnp.where(adj_matrix, local_scores, jnp.float32(-1000000000.0))
        global_scores = gQ @ gK.T * scale
        max_score = jnp.maximum(jnp.max(local_scores, axis=1, keepdims=True), jnp.maximum(global_scores, es))
        le = jnp.exp(local_scores - max_score)
        ge = jnp.exp(global_scores - max_score)
        ee = jnp.exp(es - max_score)
        denom = jnp.sum(le, axis=-1, keepdims=True) + ge + ee
        res = le / denom @ lV + ge / denom * gV + ee / denom * eV
        x_recon = jnp.maximum(res, masked_x)
        return x_recon
    x = _layernorm(x + _L0_gnn_ref(adj, x, L0_gnn_masked_x, L0_gnn_Wlq, L0_gnn_Wlk, L0_gnn_Wlv, L0_gnn_blv, L0_gnn_Wgq, L0_gnn_Wgk, L0_gnn_Wgv, L0_gnn_bgv, L0_gnn_Wes, L0_gnn_Wev, L0_gnn_bev), axis=-1)
    return x

_drawn_inputs = setup_inputs


def setup_inputs(seed=0):
    import zlib

    import numpy as np

    out = dict(_drawn_inputs(seed))
    spreads = {}
    factors = {'L0_gnn_blv': 8.0,
     'L0_gnn_Wgq': 8.0,
     'L0_gnn_Wgk': 8.0,
     'L0_gnn_Wgv': 24.336,
     'L0_gnn_bgv': 33.996,
     'L0_gnn_bev': 33.413}
    for name, (base, spread) in spreads.items():
        noise = np.random.default_rng([zlib.crc32(name.encode()), seed]).standard_normal(out[name].shape)
        drawn = base * np.exp(spread * noise) if base else spread * noise
        out[name] = jnp.asarray(drawn.astype(out[name].dtype))
    for name, factor in factors.items():
        out[name] = (out[name] * factor).astype(out[name].dtype)
    return out
```

```python
import numpy as np
import concourse.bass as bass
from concourse import mybir
from contextlib import ExitStack

F32 = mybir.dt.float32
U8 = mybir.dt.uint8
ALU = mybir.AluOpType
ACT = mybir.ActivationFunctionType
AX = mybir.AxisListType

N = 4096
D = 256
P = 128
H = D // P
TILES = N // P
GROUP = 512
GROUPS = N // GROUP
CHUNKS = GROUP // P
MASKED = -1000000000.0
SCALE = 1.0 / 16.0
EPS = 1e-05


def build(nc, x, adj, masked_x, Wlq, Wlk, Wlv, blv, Wgq, Wgk, Wgv, bgv, Wes, Wev, bev, out):
    ctx = ExitStack()
    with ctx:
        def sb(name, shape, dt=F32):
            return ctx.enter_context(nc.sbuf_tensor(name, shape, dt))

        def ps(name, shape):
            return ctx.enter_context(nc.psum_tensor(name, shape, F32))

        def sem(name):
            return ctx.enter_context(nc.semaphore(name))

        x_all = sb("x_all", [P, TILES, D])
        m_all = sb("m_all", [P, TILES, D])
        xT_all = sb("xT_all", [P, H, N])
        w = {k: sb(k, [P, H, D]) for k in ("wlq", "wlk", "wlv", "wgq", "wgk", "wgv")}
        wT = {k: sb(k + "T", [P, H, D]) for k in ("wlq", "wlk", "wgq")}
        A = sb("A", [P, H, D])
        wevx = sb("wevx", [P, H, D + 2])
        blv_b = sb("blv_b", [P, D])
        bev_b = sb("bev_b", [P, D])
        bgv_b = sb("bgv_b", [P, D])
        gV_b = sb("gV_b", [P, D])
        ident = sb("ident", [P, P])
        mean_col = sb("mean_col", [P, 1])
        eps_col = sb("eps_col", [P, 1])
        xsum = sb("xsum", [P, D])
        xbarT = sb("xbarT", [P, H])
        gKT = sb("gKT", [P, H])
        xbarB = sb("xbarB", [P, H, P])
        adj_t = sb("adj_t", [P, N], U8)
        m_t = sb("m_t", [P, D])
        mT = sb("mT", [P, H, P])
        TT = sb("TT", [P, H, P])
        Ev = sb("Ev", [P, D + 2])
        S = sb("S", [P, N])
        PT = [sb(f"PT{i}", [P, CHUNKS, P]) for i in range(2)]
        Ox = sb("Ox", [P, D])
        OxT = sb("OxT", [P, H, P])
        acc = sb("acc", [P, D])
        acc2 = sb("acc2", [P, D])
        st = sb("st", [P, 16])
        stats = sb("stats", [P, 6])
        mv = sb("mv", [P, TILES, 2])
        mv_t = sb("mv_t", [P, 2])
        var = sb("var", [P, TILES])
        std = sb("std", [P, TILES])
        rstd = sb("rstd", [P, TILES])

        bank = [ps(f"bank{i}", [P, 512]) for i in range(8)]

        s_w = sem("s_w")
        s_x = sem("s_x")
        s_m = sem("s_m")
        s_id = sem("s_id")
        s_wT = sem("s_wT")
        s_wTc = sem("s_wTc")
        s_pe_set = sem("s_pe_set")
        s_v_set = sem("s_v_set")
        s_a_set = sem("s_a_set")
        s_xt = sem("s_xt")
        s_xtc = sem("s_xtc")
        s_adj = sem("s_adj")
        s_fill = sem("s_fill")
        s_mcp = sem("s_mcp")
        s_mTp = sem("s_mTp")
        s_mT = sem("s_mT")
        s_TTp = sem("s_TTp")
        s_TT = sem("s_TT")
        s_Ep = sem("s_Ep")
        s_E = sem("s_E")
        s_S = sem("s_S")
        s_Sm = sem("s_Sm")
        s_nmax = sem("s_nmax")
        s_exp = sem("s_exp")
        s_PTp = sem("s_PTp")
        s_PT = sem("s_PT")
        s_PV = sem("s_PV")
        s_Ox = sem("s_Ox")
        s_OTp = sem("s_OTp")
        s_OT = sem("s_OT")
        s_O = sem("s_O")
        s_y = sem("s_y")
        s_chain = sem("s_chain")
        s_passed = sem("s_passed")
        s_mv = sem("s_mv")
        s_var = sem("s_var")
        s_std = sem("s_std")
        s_norm = sem("s_norm")
        s_out = sem("s_out")

        block = ctx.enter_context(nc.Block())

        half = lambda a: a.rearrange("(h p) n -> p h n", p=P)
        rows = lambda a: a.rearrange("(t p) d -> p t d", p=P)

        @block.sync
        def _(sp):
            for name, a in (("wlq", Wlq), ("wlk", Wlk), ("wgq", Wgq), ("wlv", Wlv), ("wgk", Wgk), ("wgv", Wgv)):
                sp.dma_start(w[name][:, :, :], half(a)).then_inc(s_w, 16)
            sp.dma_start(wevx[:, :, 0:D], half(Wev)).then_inc(s_w, 16)
            sp.dma_start(wevx[:, :, D:D + 1], half(Wes), allow_slow_non_contiguous=True).then_inc(s_w, 16)
            for b, a in ((blv_b, blv), (bev_b, bev), (bgv_b, bgv)):
                sp.dma_start(b[:, :], a.rearrange("(a n) -> a n", a=1).broadcast_to([P, D])).then_inc(s_w, 16)
            for q in range(4):
                ts = slice(q * TILES // 4, (q + 1) * TILES // 4)
                sp.dma_start(x_all[:, ts, :], rows(x)[:, ts, :]).then_inc(s_x, 16)
            for q in range(4):
                ts = slice(q * TILES // 4, (q + 1) * TILES // 4)
                sp.dma_start(m_all[:, ts, :], rows(masked_x)[:, ts, :]).then_inc(s_m, 16)
            sp.dma_start(adj_t[:, :], adj[0:P, :]).then_inc(s_adj, 16)
            with sp.Fori(1, TILES) as t:
                sp.wait_ge(s_Sm, t * GROUPS)
                sp.dma_start(adj_t[:, :], adj[bass.ts(t, P), :]).then_inc(s_adj, 16)
            with sp.Fori(0, TILES) as t:
                sp.wait_ge(s_norm, t + 1)
                sp.dma_start(out[bass.ts(t, P), :], x_all[:, bass.ts(t, 1), :].rearrange("p a d -> p (a d)")).then_inc(s_out, 16)
            sp.wait_ge(s_out, 16 * TILES)

        @block.gpsimd
        def _(pool):
            nc.gpsimd.memset(ident[:, :], 0.0).then_inc(s_id, 1)
            pool.wait_ge(s_id, 1)
            nc.gpsimd.affine_select(out=ident[:, :], in_=ident[:, :], compare_op=ALU.not_equal, fill=1.0,
                                    base=0, pattern=[[-1, P]], channel_multiplier=1).then_inc(s_id, 1)
            nc.gpsimd.memset(mean_col[:, :], 1.0 / N).then_inc(s_id, 1)
            nc.gpsimd.memset(eps_col[:, :], EPS).then_inc(s_id, 1)
            pool.wait_ge(s_m, 64)
            pool.wait_ge(s_id, 4)
            with pool.Fori(0, TILES) as t:
                pool.wait_ge(s_mTp, t)
                nc.gpsimd.tensor_copy(m_t[:, :], m_all[:, bass.ts(t, 1), :].rearrange("p a d -> p (a d)")).then_inc(s_mcp, 1)
                pool.wait_ge(s_PTp, t * GROUPS)
                pool.sem_inc(s_passed, 1)
                nc.gpsimd.memset(S[:, :], MASKED).then_inc(s_fill, 1)

        @block.scalar
        def _(act):
            for i, k in enumerate(("wlq", "wlk", "wgq")):
                act.wait_ge(s_wT, i + 1)
                nc.scalar.copy(wT[k][:, :, :], bank[i][:, :].rearrange("p (h d) -> p h d", h=H)).then_inc(s_wTc, 1)
            act.wait_ge(s_pe_set, 1)
            nc.scalar.mul(A[:, :, :], bank[3][:, :].rearrange("p (h d) -> p h d", h=H), SCALE).then_inc(s_a_set, 1)
            with act.Fori(0, TILES // 2) as c:
                act.wait_ge(s_xt, c + 1)
                nc.scalar.copy(xT_all[:, :, bass.ts(c, 2 * P)],
                               bank[6][:, :].rearrange("p (h k) -> p h k", h=H)).then_inc(s_xtc, 1)
            with act.Fori(0, TILES) as t:
                act.wait_ge(s_mTp, t + 1)
                nc.scalar.copy(mT[:, :, :], bank[0][:, 0:D].rearrange("p (h k) -> p h k", h=H)).then_inc(s_mT, 1)
                act.wait_ge(s_TTp, t + 1)
                nc.scalar.copy(TT[:, :, :], bank[1][:, 0:D].rearrange("p (h k) -> p h k", h=H)).then_inc(s_TT, 1)
                act.wait_ge(s_nmax, t + 1)
                nc.scalar.activation(S[:, :], S[:, :], ACT.Exp, bias=st[:, 1:2], accum_out=st[:, 2:3]).then_inc(s_exp, 1)
                nc.scalar.activation(st[:, 3:5], Ev[:, D:D + 2], ACT.Exp, bias=st[:, 1:2]).then_inc(s_exp, 1)
                for g in range(1, GROUPS, 2):
                    act.wait_ge(s_PTp, t * GROUPS + g + 1)
                    nc.scalar.copy(PT[1][:, :, :], bank[2 + g % 2][:, :].rearrange("p (c q) -> p c q", c=CHUNKS)).then_inc(s_PT, 1)
                act.wait_ge(s_OTp, t + 1)
                nc.scalar.copy(OxT[:, :, :], bank[0][:, 0:D].rearrange("p (h k) -> p h k", h=H)).then_inc(s_OT, 1)
            act.wait_ge(s_var, 1)
            nc.scalar.activation(std[:, :], var[:, :], ACT.Sqrt, bias=eps_col[:, 0:1]).then_inc(s_std, 1)

        @block.vector
        def _(dve):
            dve.wait_ge(s_x, 64)
            nc.vector.reduce_sum(xsum[:, :], x_all[:, :, :].rearrange("p t d -> p d t"), axis=AX.X).then_inc(s_v_set, 1)
            dve.wait_ge(s_pe_set, 2)
            nc.vector.tensor_copy(xbarT[:, :], bank[4][:, 0:H]).then_inc(s_v_set, 1)
            dve.wait_ge(s_v_set, 2)
            nc.vector.tensor_copy(xbarB[:, :, :], xbarT[:, :].unsqueeze(2).broadcast_to([P, H, P])).then_inc(s_v_set, 1)
            dve.wait_ge(s_pe_set, 3)
            nc.vector.tensor_copy(gKT[:, :], bank[5][:, 0:H]).then_inc(s_v_set, 1)
            dve.wait_ge(s_pe_set, 5)
            dve.wait_ge(s_w, 16 * 11)
            nc.vector.tensor_tensor(gV_b[:, :], bank[4][:, 0:D], bgv_b[:, :], ALU.add).then_inc(s_v_set, 1)
            nc.vector.tensor_scalar(wevx[:, :, D + 1], bank[5][:, 0:H], SCALE, None, ALU.mult).then_inc(s_v_set, 1)
            with dve.Fori(0, TILES) as t:
                dve.wait_ge(s_Ep, t + 1)
                nc.vector.tensor_copy(Ev[:, :], bank[7][:, 0:D + 2]).then_inc(s_E, 1)
                dve.wait_ge(s_fill, t + 1)
                dve.wait_ge(s_adj, 16 * t + 16)
                for g in range(GROUPS):
                    dve.wait_ge(s_S, t * GROUPS + g + 1)
                    dve.sem_inc(s_passed, 1)
                    nc.vector.copy_predicated(S[:, g * GROUP:(g + 1) * GROUP], adj_t[:, g * GROUP:(g + 1) * GROUP],
                                              bank[4 + g % 2][:, :]).then_inc(s_Sm, 1)
                dve.wait_ge(s_Sm, (t + 1) * GROUPS)
                nc.vector.reduce_max(st[:, 0:1], S[:, :], axis=AX.X).then_inc(s_chain, 1)
                dve.wait_ge(s_E, t + 1)
                nc.vector.reduce_max(st[:, 5:6], Ev[:, D:D + 2], axis=AX.X).then_inc(s_chain, 1)
                dve.wait_ge(s_chain, 8 * t + 2)
                nc.vector.tensor_scalar(st[:, 1:2], st[:, 0:1], st[:, 5:6], -1.0, ALU.max, ALU.mult).then_inc(s_nmax, 1)
                for g in range(0, GROUPS, 2):
                    dve.wait_ge(s_PTp, t * GROUPS + g + 1)
                    nc.vector.tensor_copy(PT[0][:, :, :], bank[2 + g % 2][:, :].rearrange("p (c q) -> p c q", c=CHUNKS)).then_inc(s_PT, 1)
                dve.wait_ge(s_PV, (t + 1) * GROUPS)
                nc.vector.tensor_copy(Ox[:, :], bank[6][:, 0:D]).then_inc(s_Ox, 1)
                dve.wait_ge(s_exp, 2 * t + 2)
                nc.vector.reduce_sum(st[:, 6:7], st[:, 2:5], axis=AX.X).then_inc(s_chain, 1)
                dve.wait_ge(s_chain, 8 * t + 3)
                nc.vector.reciprocal(st[:, 7:8], st[:, 6:7]).then_inc(s_chain, 1)
                nc.vector.tensor_tensor(acc[:, :], Ev[:, 0:D], bev_b[:, :], ALU.add).then_inc(s_chain, 1)
                dve.wait_ge(s_O, t + 1)
                dve.wait_ge(s_chain, 8 * t + 5)
                nc.vector.scalar_tensor_tensor(acc2[:, :], acc[:, :], st[:, 3:4], bank[7][:, 0:D], ALU.mult, ALU.add).then_inc(s_chain, 1)
                dve.wait_ge(s_chain, 8 * t + 6)
                nc.vector.scalar_tensor_tensor(acc[:, :], gV_b[:, :], st[:, 4:5], acc2[:, :], ALU.mult, ALU.add).then_inc(s_chain, 1)
                dve.wait_ge(s_chain, 8 * t + 7)
                nc.vector.scalar_tensor_tensor(acc2[:, :], blv_b[:, :], st[:, 2:3], acc[:, :], ALU.mult, ALU.add).then_inc(s_chain, 1)
                dve.wait_ge(s_chain, 8 * t + 8)
                m_row = m_all[:, bass.ts(t, 1), :].rearrange("p a d -> p (a d)")
                x_row = x_all[:, bass.ts(t, 1), :].rearrange("p a d -> p (a d)")
                nc.vector.scalar_tensor_tensor(acc[:, :], acc2[:, :], st[:, 7:8], m_row, ALU.mult, ALU.max).then_inc(s_y, 1)
                dve.wait_ge(s_y, 3 * t + 1)
                nc.vector.tensor_tensor(m_row, acc[:, :], x_row, ALU.add).then_inc(s_y, 1)
                dve.wait_ge(s_y, 3 * t + 2)
                dve.sem_inc(s_passed, 1)
                nc.vector.bn_stats(stats[:, :], m_row).then_inc(s_y, 1)
                dve.wait_ge(s_y, 3 * t + 3)
                dve.sem_inc(s_passed, 1)
                nc.vector.bn_aggr(mv_t[:, :], stats[:, :]).then_inc(s_mv, 1)
                dve.wait_ge(s_mv, 2 * t + 1)
                nc.vector.tensor_copy(mv[:, bass.ts(t, 1), :].rearrange("p a d -> p (a d)"), mv_t[:, :]).then_inc(s_mv, 1)
            dve.wait_ge(s_mv, 2 * TILES)
            nc.vector.tensor_copy(var[:, :], mv[:, :, 1]).then_inc(s_var, 1)
            dve.wait_ge(s_std, 1)
            nc.vector.reciprocal(rstd[:, :], std[:, :]).then_inc(s_std, 1)
            dve.wait_ge(s_std, 2)
            with dve.Fori(0, TILES) as t:
                nc.vector.tensor_scalar(x_all[:, bass.ts(t, 1), :].rearrange("p a d -> p (a d)"),
                                        m_all[:, bass.ts(t, 1), :].rearrange("p a d -> p (a d)"),
                                        mv[:, bass.ts(t, 1), 0], rstd[:, bass.ts(t, 1)],
                                        ALU.subtract, ALU.mult).then_inc(s_norm, 1)

        @block.tensor
        def _(pe):
            pe.wait_ge(s_id, 4)
            pe.wait_ge(s_w, 16 * 11)
            for i, k in enumerate(("wlq", "wlk", "wgq")):
                for d in range(H):
                    for c in range(H):
                        last = nc.tensor.transpose(bank[i][:, c * D + d * P:c * D + (d + 1) * P],
                                                   w[k][:, d, c * P:(c + 1) * P], ident[:, :])
                last.then_inc(s_wT, 1)
            pe.wait_ge(s_wTc, 2)
            for d in range(H):
                for c in range(H):
                    last = nc.tensor.matmul(bank[3][:, d * D:(d + 1) * D], wT["wlq"][:, c, d * P:(d + 1) * P],
                                            wT["wlk"][:, c, :], start=(c == 0), stop=(c == H - 1))
            last.then_inc(s_pe_set, 1)
            pe.wait_ge(s_v_set, 1)
            for h in range(H):
                last = nc.tensor.matmul(bank[4][:, h:h + 1], xsum[:, h * P:(h + 1) * P], mean_col[:, :], start=True, stop=True)
            last.then_inc(s_pe_set, 1)
            pe.wait_ge(s_v_set, 2)
            for c in range(H):
                for h in range(H):
                    last = nc.tensor.matmul(bank[5][:, c:c + 1], w["wgk"][:, h, c * P:(c + 1) * P], xbarT[:, h:h + 1],
                                            start=(h == 0), stop=(h == H - 1))
            last.then_inc(s_pe_set, 1)
            pe.wait_ge(s_v_set, 3)
            for h in range(H):
                last = nc.tensor.matmul(bank[4][:, 0:D], xbarB[:, h, :], w["wgv"][:, h, :], start=(h == 0), stop=(h == H - 1))
            last.then_inc(s_pe_set, 1)
            pe.wait_ge(s_v_set, 4)
            pe.wait_ge(s_wTc, 3)
            for h in range(H):
                for c in range(H):
                    last = nc.tensor.matmul(bank[5][:, h:h + 1], wT["wgq"][:, c, h * P:(h + 1) * P], gKT[:, c:c + 1],
                                            start=(c == 0), stop=(c == H - 1))
            last.then_inc(s_pe_set, 1)
            for c in range(TILES // 2):
                if c >= 1:
                    pe.wait_ge(s_xtc, c)
                for j in range(2):
                    for h in range(H):
                        last = nc.tensor.transpose(bank[6][:, h * 2 * P + j * P:h * 2 * P + (j + 1) * P],
                                                   x_all[:, 2 * c + j, h * P:(h + 1) * P], ident[:, :])
                last.then_inc(s_xt, 1)
            pe.wait_ge(s_xtc, TILES // 2)
            pe.wait_ge(s_v_set, 6)
            pe.wait_ge(s_a_set, 1)
            with pe.Fori(0, TILES) as t:
                pe.wait_ge(s_mcp, t + 1)
                for h in range(H):
                    last = nc.tensor.transpose(bank[0][:, h * P:(h + 1) * P], m_t[:, h * P:(h + 1) * P], ident[:, :])
                last.then_inc(s_mTp, 1)
                pe.wait_ge(s_mT, t + 1)
                for o in range(H):
                    for h in range(H):
                        last = nc.tensor.matmul(bank[1][:, o * P:(o + 1) * P], A[:, h, o * P:(o + 1) * P], mT[:, h, :],
                                                start=(h == 0), stop=(h == H - 1))
                last.then_inc(s_TTp, 1)
                pe.wait_ge(s_y, 3 * t)
                for h in range(H):
                    last = nc.tensor.matmul(bank[7][:, 0:D + 2], mT[:, h, :], wevx[:, h, :], start=(h == 0), stop=(h == H - 1))
                last.then_inc(s_Ep, 1)
                pe.wait_ge(s_TT, t + 1)
                for g in range(GROUPS):
                    if g >= 2:
                        pe.wait_ge(s_Sm, t * GROUPS + g - 1)
                    else:
                        pe.wait_ge(s_Sm, t * GROUPS)
                    for h in range(H):
                        last = nc.tensor.matmul(bank[4 + g % 2][:, :], TT[:, h, :], xT_all[:, h, g * GROUP:(g + 1) * GROUP],
                                                start=(h == 0), stop=(h == H - 1))
                    last.then_inc(s_S, 1)

                def transposes(g):
                    if g >= 2:
                        pe.wait_ge(s_PT, t * GROUPS + g - 1)
                    for c in range(CHUNKS):
                        k = g * GROUP + c * P
                        last = nc.tensor.transpose(bank[2 + g % 2][:, c * P:(c + 1) * P], S[:, k:k + P], ident[:, :])
                    last.then_inc(s_PTp, 1)

                def products(g):
                    pe.wait_ge(s_PT, t * GROUPS + g + 1)
                    for c in range(CHUNKS):
                        last = nc.tensor.matmul(bank[6][:, 0:D], PT[g % 2][:, c, :], x_all[:, g * CHUNKS + c, :],
                                                start=(g == 0 and c == 0), stop=(g == GROUPS - 1 and c == CHUNKS - 1))
                    last.then_inc(s_PV, 1)

                pe.wait_ge(s_exp, 2 * t + 1)
                transposes(0)
                for g in range(GROUPS):
                    products(g)
                    if g + 1 < GROUPS:
                        transposes(g + 1)
                pe.wait_ge(s_Ox, t + 1)
                for h in range(H):
                    last = nc.tensor.transpose(bank[0][:, h * P:(h + 1) * P], Ox[:, h * P:(h + 1) * P], ident[:, :])
                last.then_inc(s_OTp, 1)
                pe.wait_ge(s_OT, t + 1)
                for h in range(H):
                    last = nc.tensor.matmul(bank[7][:, 0:D], OxT[:, h, :], w["wlv"][:, h, :], start=(h == 0), stop=(h == H - 1))
                last.then_inc(s_O, 1)


_INS = ["x", "adj", "L0_gnn_masked_x", "L0_gnn_Wlq", "L0_gnn_Wlk", "L0_gnn_Wlv", "L0_gnn_blv", "L0_gnn_Wgq",
        "L0_gnn_Wgk", "L0_gnn_Wgv", "L0_gnn_bgv", "L0_gnn_Wes", "L0_gnn_Wev", "L0_gnn_bev"]


def kernel(**inputs):
    import concourse.bacc as bacc
    from concourse.bass_utils import run_bass_kernel_spmd

    nc = bacc.Bacc("TRN2", target_bir_lowering=False, num_devices=1)
    arrays, args = {}, []
    for name in _INS:
        a = np.ascontiguousarray(inputs[name])
        arrays[f"in_{name}"] = a
        args.append(nc.dram_tensor(f"in_{name}", a.shape, mybir.dt.from_np(a.dtype), kind="ExternalInput").ap())
    args.append(nc.dram_tensor("out_rows", (N, D), F32, kind="ExternalOutput").ap())
    build(nc, *args)
    r = run_bass_kernel_spmd(nc, [arrays], core_ids=[0])
    return r.results[0]["out_rows"]
```

```python
import numpy as np
import concourse.bass as bass
from concourse import mybir
from contextlib import ExitStack

F32 = mybir.dt.float32
F16 = mybir.dt.float16
I32 = mybir.dt.int32
U32 = mybir.dt.uint32
U16 = mybir.dt.uint16
U8 = mybir.dt.uint8
ALU = mybir.AluOpType
ACT = mybir.ActivationFunctionType
AX = mybir.AxisListType

N = 4096
D = 256
P = 128
H = D // P
TILES = N // P
GROUP = 512
GROUPS = N // GROUP
CHUNKS = GROUP // P
MASKED = -1000000000.0
UNLISTED = -1.0e30
SURE = 9.0e8
SCALE = 1.0 / 16.0
EPS = 1e-05

G = 8
NG = TILES // G
PAIRS = TILES // 2
WORDS = 256
SLOTS = 16
LEVELS = 2
LISTED = GROUP - P
LC = LISTED // P
CENTRE = 2048.0
EXPONENT = 0x7F800000
STEPS_OF_GROUP = 61
AHEAD = 4


def build(nc, x, adj, masked_x, Wlq, Wlk, Wlv, blv, Wgq, Wgk, Wgv, bgv, Wes, Wev, bev, out):
    ctx = ExitStack()
    with ctx:
        def sb(name, shape, dt=F32):
            return ctx.enter_context(nc.sbuf_tensor(name, shape, dt))

        def sem(name):
            return ctx.enter_context(nc.semaphore(name))

        half = lambda a: a.rearrange("(h p) n -> p h n", p=P)
        rows = lambda a: a.rearrange("(t p) d -> p t d", p=P)
        halves = lambda a: a.rearrange("p (h k) -> p h k", h=H)
        one = lambda a: a.rearrange("p a d -> p (a d)")

        T_all = sb("T_all", [P, TILES, H, P])
        E_all = sb("E_all", [P, TILES, D + 2])
        mask_own = sb("mask_own", [P, TILES, P], U8)
        mask_list = sb("mask_list", [P, TILES, LISTED], F16)
        idx_all = sb("idx_all", [P, TILES, LC], U32)
        em_all = sb("em_all", [P, TILES, 1])
        negm_all = sb("negm_all", [P, TILES, 1])
        bad_all = sb("bad_all", [P, NG, 3])
        w = {k: sb(k, [P, H, D]) for k in ("wlq", "wlk", "wlv", "wgq", "wgk", "wgv")}
        xT = [sb(f"xT{i}", [P, H, GROUP]) for i in range(2)]
        wT = {k: halves(v) for k, v in (("wlq", xT[0][:, 0, :]), ("wlk", xT[0][:, 1, :]), ("wgq", xT[1][:, 0, :]))}
        A = sb("A", [P, H, D])
        wevx = sb("wevx", [P, H, D + 2])
        blv_b = sb("blv_b", [P, D])
        bev_b = sb("bev_b", [P, D])
        bgv_b = sb("bgv_b", [P, D])
        gV_b = sb("gV_b", [P, D])
        ident = sb("ident", [P, P])
        verdict = sb("verdict", [P, 4])
        general_i = sb("general_i", [P, 1], I32)
        before = sb("before", [P, P])
        ones = sb("ones", [P, P])
        mean_sq = sb("mean_sq", [P, P])
        eps_col = sb("eps_col", [P, 1])
        power = sb("power", [P, 1])
        word_row = sb("word_row", [P, WORDS])
        place_row = sb("place_row", [P, LISTED], F16)
        place_col = sb("place_col", [P, G * LC, 2])
        slot_row = sb("slot_row", [P, SLOTS // 2])
        zero_blk = sb("zero_blk", [P, P // 4], U32)
        xbarB = sb("xbarB", [P, H, P])
        gKT = sb("gKT", [P, H])
        adj_p = [sb(f"adj_p{i}", [P, 2, N], U8) for i in range(2)]
        or1 = sb("or1", [P, 2, 512], U32)
        or2 = sb("or2", [P, 2, 256], U32)
        or3 = sb("or3", [P, 2, 128], U32)
        code = sb("code", [P, 2, WORDS])
        top = sb("top", [P, G, SLOTS])
        topi = sb("topi", [P, G * SLOTS], I32)
        place2 = sb("place2", [P, G * SLOTS], I32)
        word_i = sb("word_i", [P, G * SLOTS], I32)
        bits = sb("bits", [P, LEVELS + 1, G * SLOTS])
        high = sb("high", [P, LEVELS, G * SLOTS], I32)
        kx = sb("kx", [P, LEVELS, G * SLOTS], I32)
        ku = sb("ku", [P, LEVELS, G * SLOTS], I32)
        kv = sb("kv", [P, LEVELS, G * SLOTS])
        cand = sb("cand", [P, LEVELS, G * SLOTS])
        keys1 = sb("keys1", [P, G, SLOTS])
        some = sb("some", [P, G, SLOTS])
        n2 = sb("n2", [P, G, 2])
        n_row = sb("n_row", [P, G])
        off = sb("off", [P, G])
        end = sb("end", [P, G])
        mxt = sb("mxt", [P, G])
        R = sb("R", [P, G, SLOTS + 2], F16)
        geA = sb("geA", [P, 2, LISTED], F16)
        geB = sb("geB", [P, 2, LISTED], F16)
        rel = sb("rel", [P, G * LC, 2])
        hit = sb("hit", [P, G * LC, SLOTS])
        hitk = sb("hitk", [P, G * LC, SLOTS])
        keyf = sb("keyf", [P, G * LC])
        keyg = sb("keyg", [P, G * LC])
        m_t = [sb(f"m_t{i}", [P, D]) for i in range(2)]
        mT = [sb(f"mT{i}", [P, H, P]) for i in range(2)]
        idx_t = [sb(f"idx_t{i}", [P, LC], U32) for i in range(2)]
        TT = [sb(f"TT{i}", [P, H * P]) for i in range(2)]
        x_cat = [adj_p[i // 2][:, i % 2, :].bitcast(F32).rearrange("p (c d) -> p c d", c=CHUNKS) for i in range(AHEAD)]
        m_row = [sb(f"m_row{i}", [P, D]) for i in range(AHEAD)]
        bias = [sb(f"bias{i}", [P, GROUP]) for i in range(2)]
        S = [sb(f"S{i}", [P, GROUP]) for i in range(2)]
        PT = [sb(f"PT{i}", [P, CHUNKS, P]) for i in range(2)]
        OT = [sb(f"OT{i}", [P, H, P]) for i in range(2)]
        mx = [sb(f"mx{i}", [P, 1]) for i in range(2)]
        negm = [sb(f"negm{i}", [P, 1]) for i in range(2)]
        st = [sb(f"st{i}", [P, 8]) for i in range(2)]
        acc = [sb(f"acc{i}", [P, D]) for i in range(2)]
        acc2 = [sb(f"acc2{i}", [P, D]) for i in range(2)]
        Eb = [sb(f"Eb{i}", [P, D]) for i in range(2)]
        y = [sb(f"y{i}", [P, D]) for i in range(2)]
        o_t = [sb(f"o_t{i}", [P, D]) for i in range(2)]
        stats = [sb(f"stats{i}", [P, 6]) for i in range(2)]
        mv = [sb(f"mv{i}", [P, 2]) for i in range(2)]
        ve = [sb(f"ve{i}", [P, 1]) for i in range(2)]
        rstd = [sb(f"rstd{i}", [P, 1]) for i in range(2)]

        bank = [ctx.enter_context(nc.psum_tensor(f"bank{i}", [P, 512], F32)) for i in range(8)]

        S_ = {}

        def s(name):
            if name not in S_:
                S_[name] = sem("s_" + name)
            return S_[name]

        for n in ("w w1 x const gconst own zeroed or1 or2 or3 code top decode counts offs R masks G idx "
                  "wT wTc prod prodc xsum passed_v passed_p mTp mT TTp TT Ep E em "
                  "idxc TTc bias xTp xT Sp Sm negm exp PTp PT OTp OT Wp ep Eb y y2 st pw norm verdict verdictp").split():
            s(n)

        nW = 8 * 16

        def loaded(name, t, buf, of, dmas=1):
            return 16 * dmas // of * (t - buf) + 16 * dmas

        for n in ["adj", "mt", "out"]:
            for i in range(2):
                s(f"{n}{i}")
        for n in ["xt", "m", "gath"]:
            for i in range(AHEAD):
                s(f"{n}{i}")

        block_ctx = nc.Block()
        block = block_ctx.__enter__()

        @block.sync
        def _(sp):
            def load_pair(p, buf):
                sp.dma_start(adj_p[buf][:, :, :], adj[bass.ts(p, 2 * P), :].rearrange("(j p) n -> p j n", p=P)).then_inc(s(f"adj{buf}"), 16)

            load_pair(0, 0)
            for name, a in (("wlq", Wlq), ("wlk", Wlk), ("wgq", Wgq)):
                sp.dma_start(w[name][:, :, :], half(a)).then_inc(s("w1"), 16)
            load_pair(1, 1)
            for q in range(4):
                ts = slice(q * TILES // 4, (q + 1) * TILES // 4)
                sp.dma_start(E_all[:, ts, 0:D], rows(x)[:, ts, :]).then_inc(s("x"), 16)
            for name, a in (("wlv", Wlv), ("wgk", Wgk), ("wgv", Wgv)):
                sp.dma_start(w[name][:, :, :], half(a)).then_inc(s("w"), 16)
            sp.dma_start(wevx[:, :, 0:D], half(Wev)).then_inc(s("w"), 16)
            sp.dma_start(wevx[:, :, D:D + 1], half(Wes), allow_slow_non_contiguous=True).then_inc(s("w"), 16)
            for b, a in ((blv_b, blv), (bev_b, bev), (bgv_b, bgv)):
                sp.dma_start(b[:, :], a.rearrange("(a n) -> a n", a=1).broadcast_to([P, D])).then_inc(s("w"), 16)
            with sp.Fori(1, PAIRS // 2) as i:
                for j in range(2):
                    sp.wait_ge(s("or1"), 2 * i + j - 1)
                    load_pair(2 * i + j, j)

            def x_in(t, buf):
                sp.dma_start(x_cat[buf][:, 0, :], x[bass.ts(t, P), :]).then_inc(s(f"xt{buf}"), 16)
                sp.dma_start(m_row[buf][:, :], masked_x[bass.ts(t, P), :]).then_inc(s(f"m{buf}"), 16)

            def rows_out(t, b):
                sp.wait_ge(s("norm"), t + 1)
                sp.dma_start(out[bass.ts(t, P), :], o_t[b][:, :]).then_inc(s(f"out{b}"), 16)

            sp.wait_ge(s("or1"), PAIRS)
            for t in range(AHEAD):
                x_in(t, t)
            with sp.Fori(1, TILES // AHEAD) as i:
                for j in range(AHEAD):
                    rows_out(AHEAD * (i - 1) + j, j % 2)
                    x_in(AHEAD * i + j, j)
            for t in range(TILES - AHEAD, TILES):
                rows_out(t, t % 2)
            for b in range(2):
                sp.wait_ge(s(f"out{b}"), 8 * TILES)

        @block.gpsimd
        def _(pool):
            g_ = nc.gpsimd
            g_.memset(ident[:, :], 0.0).then_inc(s("gconst"), 1)
            g_.memset(ones[:, :], 1.0).then_inc(s("gconst"), 1)
            g_.memset(zero_blk[:, :], 0).then_inc(s("gconst"), 1)
            g_.iota(word_row[:, :], [[1, WORDS]], base=0, channel_multiplier=0, allow_small_or_imprecise_dtypes=True).then_inc(s("gconst"), 1)
            pool.wait_ge(s("gconst"), 4)

            def own_block(p, j, buf):
                t = 2 * p + j
                blk = adj_p[buf][:, j, bass.ts(t, P)]
                g_.tensor_copy(one(mask_own[:, bass.ts(t, 1), :]), blk).then_inc(s("own"), 1)
                pool.wait_ge(s("own"), t + 1)
                pool.sem_inc(s("passed_p"), 1)
                g_.tensor_copy(adj_p[buf][:, j, :].bitcast(U32)[:, bass.ts(t, P // 4)], zero_blk[:, :]).then_inc(s("zeroed"), 1)

            def pairs(g):
                for i in range(G // 2):
                    p = g * (G // 2) + i
                    pool.wait_ge(s(f"adj{i % 2}"), loaded("adj", p, i % 2, 2))
                    pool.sem_inc(s("passed_p"), 1)
                    for j in range(2):
                        own_block(p, j, i % 2)

            pool.wait_ge(s("adj0"), 16)
            for j in range(2):
                own_block(0, j, 0)
            g_.affine_select(out=ident[:, :], in_=ident[:, :], compare_op=ALU.not_equal, fill=1.0,
                             base=0, pattern=[[-1, P]], channel_multiplier=1).then_inc(s("const"), 1)
            g_.affine_select(out=before[:, :], in_=ones[:, :], compare_op=ALU.is_gt, fill=0.0,
                             base=0, pattern=[[1, P]], channel_multiplier=-1).then_inc(s("const"), 1)
            g_.memset(mean_sq[:, :], 1.0 / N).then_inc(s("const"), 1)
            g_.memset(eps_col[:, :], EPS).then_inc(s("const"), 1)
            g_.memset(power[:, :], -0.5).then_inc(s("const"), 1)
            g_.iota(place_row[:, :], [[1, LISTED]], base=0, channel_multiplier=0, allow_small_or_imprecise_dtypes=True).then_inc(s("const"), 1)
            g_.iota(place_col[:, :, :], [[0, G], [P, LC], [0, 2]], base=0, channel_multiplier=1, allow_small_or_imprecise_dtypes=True).then_inc(s("const"), 1)
            g_.iota(slot_row[:, :], [[1, SLOTS // 2]], base=0, channel_multiplier=0, allow_small_or_imprecise_dtypes=True).then_inc(s("const"), 1)
            for p in range(1, G // 2):
                pool.wait_ge(s(f"adj{p % 2}"), loaded("adj", p, p % 2, 2))
                for j in range(2):
                    own_block(p, j, p % 2)
            pool.wait_ge(s("x"), 64)
            n, k = TILES // 2, 0
            while n:
                g_.tensor_tensor(E_all[:, 0:n, 0:D], E_all[:, 0:n, 0:D], E_all[:, n:2 * n, 0:D], ALU.add).then_inc(s("xsum"), 1)
                k += 1
                pool.wait_ge(s("xsum"), k)
                n //= 2
            with pool.Fori(1, NG) as g:
                pairs(g)

            def fetch(t, buf, b):
                g_.tensor_copy(idx_t[b][:, :], one(idx_all[:, bass.ts(t, 1), :])).then_inc(s("idxc"), 1)
                g_.tensor_copy(TT[b][:, :], T_all[:, bass.ts(t, 1), :, :].rearrange("p a h k -> p (a h k)")).then_inc(s("TTc"), 1)
                pool.wait_ge(s("idxc"), t + 1)
                pool.sem_inc(s("passed_p"), 1)
                for c in range(LC):
                    g_.indirect_dma_start(out=x_cat[buf][:, 1 + c, :], out_offset=None, in_=x,
                                          in_offset=bass.IndirectOffsetOnAxis(ap=idx_t[b][:, c:c + 1], axis=0),
                                          bounds_check=N - 1).then_inc(s(f"gath{buf}"), 16)

            def external(t, b):
                g_.tensor_tensor(Eb[b][:, :], one(E_all[:, bass.ts(t, 1), 0:D]), bev_b[:, :], ALU.add).then_inc(s("Eb"), 1)

            def inverse_deviation(t, b):
                pool.wait_ge(s("st"), 2 * t + 2)
                g_.tensor_tensor(ve[b][:, :], mv[b][:, 1:2], eps_col[:, :], ALU.add).then_inc(s("pw"), 1)
                pool.wait_ge(s("pw"), 2 * t + 1)
                g_.tensor_tensor(rstd[b][:, :], ve[b][:, :], power[:, :], ALU.pow).then_inc(s("pw"), 1)

            pool.wait_ge(s("idx"), NG)
            pool.wait_ge(s("TT"), TILES)
            pool.wait_ge(s("E"), TILES)
            fetch(0, 0, 0)
            external(0, 0)
            fetch(1, 1, 1)
            pool.wait_ge(s("Sp"), 1)
            pool.wait_ge(s("gath0"), 48)
            pool.sem_inc(s("passed_p"), 1)
            fetch(2, 2, 0)

            def step(t, j, first=False, last=0):
                if last < 3:
                    if not first:
                        pool.wait_ge(s("y"), t)
                    external(t + 1, (j + 1) % 2)
                if last == 0:
                    pool.wait_ge(s("Sp"), t + 2)
                    n = (j + 1) % AHEAD
                    pool.wait_ge(s(f"gath{n}"), loaded("gath", t + 1, n, AHEAD, LC))
                    if not first:
                        pool.wait_ge(s("OTp"), t)
                    pool.sem_inc(s("passed_p"), 1)
                    fetch(t + 3, (j + 3) % AHEAD, (j + 1) % 2)
                inverse_deviation(t, j % 2)

            step(0, 0, first=True)
            for t in range(1, AHEAD):
                step(t, t)
            with pool.Fori(1, TILES // AHEAD - 1) as i:
                for j in range(AHEAD):
                    step(AHEAD * i + j, j)
            for j in range(AHEAD):
                t = TILES - AHEAD + j
                step(t, j, last=max(0, t + 4 - TILES))

        @block.scalar
        def _(act):
            a_ = nc.scalar

            def m_in(t, b):
                act.dma_start(m_t[b][:, :], masked_x[bass.ts(t, P), :]).then_inc(s(f"mt{b}"), 16)

            m_in(0, 0)
            m_in(1, 1)
            for i, k in enumerate(("wlq", "wlk", "wgq")):
                act.wait_ge(s("wT"), i + 1)
                a_.copy(wT[k][:, :, :], halves(bank[5 + i][:, :])).then_inc(s("wTc"), 1)
            act.wait_ge(s("prod"), 1)
            a_.mul(A[:, :, :], halves(bank[3][:, :]), SCALE).then_inc(s("prodc"), 1)
            act.wait_ge(s("prod"), 2)
            a_.copy(xbarB[:, :, :], halves(bank[5][:, 0:H * P])).then_inc(s("prodc"), 1)
            act.wait_ge(s("prod"), 3)
            a_.copy(gKT[:, :], bank[6][:, 0:H]).then_inc(s("prodc"), 1)
            act.wait_ge(s("prod"), 4)
            a_.copy(gV_b[:, :], bank[7][:, 0:D]).then_inc(s("prodc"), 1)
            act.wait_ge(s("prod"), 5)
            act.wait_ge(s("w"), nW)
            a_.mul(wevx[:, :, D + 1], bank[5][:, 0:H], SCALE).then_inc(s("prodc"), 1)

            def prologue(t, b, more=True):
                act.wait_ge(s("mTp"), t + 1)
                a_.copy(mT[b][:, :, :], halves(bank[0][:, 0:H * P])).then_inc(s("mT"), 1)
                if more:
                    m_in(t + 2, b)
                act.wait_ge(s("TTp"), t + 1)
                a_.copy(T_all[:, bass.ts(t, 1), :, :].rearrange("p a h k -> p (a h k)"), bank[1][:, 0:H * P]).then_inc(s("TT"), 1)
                act.wait_ge(s("Ep"), t + 1)
                a_.copy(one(E_all[:, bass.ts(t, 1), :]), bank[2][:, 0:D + 2]).then_inc(s("E"), 1)

            with act.Fori(0, TILES // 2 - 1) as i:
                for j in range(2):
                    prologue(2 * i + j, j)
            for j in range(2):
                prologue(TILES - 2 + j, j, more=False)

            def biases(t, b):
                a_.activation(bias[b][:, 0:P], one(mask_own[:, bass.ts(t, 1), :]), ACT.Copy, scale=-UNLISTED, bias=UNLISTED).then_inc(s("bias"), 1)
                a_.activation(bias[b][:, P:GROUP], one(mask_list[:, bass.ts(t, 1), :]), ACT.Copy, scale=-UNLISTED, bias=UNLISTED).then_inc(s("bias"), 1)

            def x_transposed(t, b):
                for h in range(H):
                    act.wait_ge(s("xTp"), 2 * t + h + 1)
                    a_.copy(xT[b][:, h, :], bank[h][:, :]).then_inc(s("xT"), 1)

            def exps(t, b):
                act.wait_ge(s("negm"), t + 1)
                a_.activation(S[b][:, :], S[b][:, :], ACT.Exp, bias=negm[b][:, 0:1], accum_out=st[b][:, 0:1]).then_inc(s("exp"), 1)
                a_.activation(st[b][:, 1:3], one(E_all[:, bass.ts(t, 1), D:D + 2]), ACT.Exp, bias=negm[b][:, 0:1]).then_inc(s("exp"), 1)

            act.wait_ge(s("idx"), NG)
            act.wait_ge(s("E"), TILES)
            biases(0, 0)
            x_transposed(0, 0)
            biases(1, 1)
            x_transposed(1, 1)
            exps(0, 0)

            def step(t, j, first=False, last=0):
                b = j % 2
                if last < 2:
                    act.wait_ge(s("Sm"), t + 1)
                    biases(t + 2, b)
                act.wait_ge(s("OTp"), t + 1)
                a_.copy(OT[b][:, :, :], halves(bank[4][:, 0:H * P])).then_inc(s("OT"), 1)
                if last < 2:
                    x_transposed(t + 2, b)
                if last < 3:
                    if not first:
                        act.wait_ge(s("y"), t)
                    exps(t + 1, (b + 1) % 2)

            step(0, 0, first=True)
            for t in range(1, AHEAD):
                step(t, t)
            with act.Fori(1, TILES // AHEAD - 1) as i:
                for j in range(AHEAD):
                    step(AHEAD * i + j, j)
            for j in range(AHEAD):
                t = TILES - AHEAD + j
                step(t, j, last=max(0, t + 4 - TILES))

        @block.vector
        def _(dve):
            v_ = nc.vector
            STEPS = [0]

            def lists(g, first=False):
                for i in range(G // 2):
                    p = g * (G // 2) + i
                    a = adj_p[i % 2][:, :, :].bitcast(U32)
                    dve.wait_ge(s("zeroed"), 2 * p + 2)
                    v_.scalar_tensor_tensor(or1[:, :, :], a[:, :, 512:1024], 4, a[:, :, 0:512],
                                            ALU.logical_shift_left, ALU.bitwise_or).then_inc(s("or1"), 1)
                    dve.wait_ge(s("or1"), p + 1)
                    v_.scalar_tensor_tensor(or2[:, :, :], or1[:, :, 256:512], 2, or1[:, :, 0:256],
                                            ALU.logical_shift_left, ALU.bitwise_or).then_inc(s("or2"), 1)
                    dve.wait_ge(s("or2"), p + 1)
                    v_.scalar_tensor_tensor(or3[:, :, :], or2[:, :, 128:256], 1, or2[:, :, 0:128],
                                            ALU.logical_shift_left, ALU.bitwise_or).then_inc(s("or3"), 1)
                    dve.wait_ge(s("or3"), p + 1)
                    v_.scalar_tensor_tensor(code[:, :, :], or3[:, :, :].bitcast(U16), 256.0,
                                            word_row[:, :].unsqueeze(1).broadcast_to([P, 2, WORDS]),
                                            ALU.mult, ALU.add).then_inc(s("code"), 1)
                    dve.wait_ge(s("code"), p + 1)
                    dve.sem_inc(s("passed_v"), 1)
                    for j in range(2):
                        for h in range(2):
                            v_.max(top[:, 2 * i + j, h * 8:h * 8 + 8], code[:, j, h * P:(h + 1) * P]).then_inc(s("top"), 1)
                base, k = g * STEPS_OF_GROUP, 0
                flat = lambda a: a.rearrange("p t s -> p (t s)")
                dve.wait_ge(s("top"), (g + 1) * 2 * G)
                v_.tensor_copy(topi[:, :], flat(top[:, :, :])).then_inc(s("decode"), 1)
                dve.wait_ge(s("decode"), base + 1)
                v_.tensor_scalar(word_i[:, :], topi[:, :], 8, None, ALU.logical_shift_right).then_inc(s("decode"), 1)
                v_.tensor_scalar(place2[:, :], topi[:, :], 255, 1, ALU.bitwise_and, ALU.logical_shift_left).then_inc(s("decode"), 1)
                dve.wait_ge(s("decode"), base + 2)
                v_.tensor_scalar(bits[:, 0, :], word_i[:, :], 2.0, None, ALU.mult).then_inc(s("decode"), 1)
                for l in range(LEVELS):
                    dve.wait_ge(s("decode"), base + 4 + 2 * l)
                    v_.tensor_scalar(high[:, l, :], bits[:, l, :].bitcast(I32), EXPONENT, None, ALU.bitwise_and).then_inc(s("decode"), 1)
                    dve.wait_ge(s("decode"), base + 5 + 2 * l)
                    v_.tensor_tensor(bits[:, l + 1, :], bits[:, l, :], high[:, l, :].bitcast(F32), ALU.subtract).then_inc(s("decode"), 1)
                k = 4 + 2 * LEVELS
                dve.wait_ge(s("decode"), base + k)
                raw = bits[:, 0:LEVELS, :].bitcast(I32)
                v_.tensor_scalar(kx[:, :, :], raw, 14, 0xE00, ALU.logical_shift_right, ALU.bitwise_and).then_inc(s("decode"), 1)
                v_.tensor_scalar(ku[:, :, :], raw, 26, 1, ALU.logical_shift_right, ALU.bitwise_and).then_inc(s("decode"), 1)
                v_.tensor_scalar(kv[:, :, :], bits[:, 0:LEVELS, :], 1.0, None, ALU.min).then_inc(s("decode"), 1)
                dve.wait_ge(s("decode"), base + k + 2)
                v_.tensor_tensor(high[:, :, :], kx[:, :, :], ku[:, :, :], ALU.bitwise_or).then_inc(s("decode"), 1)
                dve.wait_ge(s("decode"), base + k + 4)
                v_.tensor_tensor(kx[:, :, :], high[:, :, :], place2[:, :].unsqueeze(1).broadcast_to([P, LEVELS, G * SLOTS]), ALU.bitwise_or).then_inc(s("decode"), 1)
                dve.wait_ge(s("decode"), base + k + 5)
                v_.scalar_tensor_tensor(cand[:, :, :], kx[:, :, :], 1.0, kv[:, :, :], ALU.add, ALU.mult).then_inc(s("decode"), 1)
                k += 6
                dve.wait_ge(s("decode"), base + k)
                dve.sem_inc(s("passed_v"), 1)
                for t in range(G):
                    for h in range(2):
                        c0 = t * SLOTS + h * 8
                        v_.max(keys1[:, t, h * 8:h * 8 + 8], cand[:, :, c0:c0 + 8]).then_inc(s("decode"), 1)
                k += 2 * G
                dve.wait_ge(s("decode"), base + k)
                v_.tensor_scalar(some[:, :, :], keys1[:, :, :], 1.0, None, ALU.min).then_inc(s("decode"), 1)
                v_.reduce_max(one(bad_all[:, bass.ts(g, 1), 0:1]), keys1[:, :, :].rearrange("p t (h e) -> p (t h) e", h=2)[:, :, 7:8].rearrange("p a b -> p (a b)"), axis=AX.X).then_inc(s("decode"), 1)
                v_.reduce_max(one(bad_all[:, bass.ts(g, 1), 1:2]), bits[:, LEVELS, :], axis=AX.X).then_inc(s("decode"), 1)
                dve.wait_ge(s("decode"), base + k + 1)
                v_.reduce_sum(n2[:, :, :].rearrange("p t h -> p (t h)"), some[:, :, :].rearrange("p t (h e) -> p (t h) e", h=2), axis=AX.X).then_inc(s("decode"), 1)
                dve.wait_ge(s("decode"), base + k + 4)
                v_.tensor_tensor(n_row[:, :], n2[:, :, 0], n2[:, :, 1], ALU.add).then_inc(s("counts"), 1)
                v_.scalar_tensor_tensor(R[:, :, 0:SLOTS], keys1[:, :, :], -CENTRE, some[:, :, :], ALU.add, ALU.mult).then_inc(s("decode"), 1)
                dve.wait_ge(s("offs"), g + 1)
                v_.tensor_copy(off[:, :], bank[3][:, 0:G]).then_inc(s("decode"), 1)
                v_.tensor_tensor(end[:, :], bank[3][:, 0:G], n_row[:, :], ALU.add).then_inc(s("decode"), 1)
                v_.tensor_copy(R[:, :, SLOTS], bank[3][:, 0:G]).then_inc(s("decode"), 1)
                v_.tensor_tensor(R[:, :, SLOTS + 1], bank[3][:, 0:G], n2[:, :, 0], ALU.add).then_inc(s("R"), 1)
                v_.tensor_scalar(mxt[:, :], bank[3][:, G:2 * G], -float(LISTED), None, ALU.add).then_inc(s("decode"), 1)
                k += 9
                dve.wait_ge(s("decode"), base + k)
                v_.reduce_max(one(bad_all[:, bass.ts(g, 1), 2:3]), mxt[:, :], axis=AX.X).then_inc(s("decode"), 1)
                k += 1
                for t in range(G):
                    if t >= 2:
                        dve.wait_ge(s("masks"), g * G + t - 1)
                    elif not first:
                        dve.wait_ge(s("masks"), g * G + t - 1)
                    v_.tensor_scalar(geA[:, t % 2, :], place_row[:, :], off[:, t:t + 1], None, ALU.is_ge).then_inc(s("decode"), 1)
                    v_.tensor_scalar(geB[:, t % 2, :], place_row[:, :], end[:, t:t + 1], None, ALU.is_ge).then_inc(s("decode"), 1)
                    k += 2
                    dve.wait_ge(s("decode"), base + k)
                    v_.tensor_tensor(one(mask_list[:, bass.ts(g * G + t, 1), :]), geA[:, t % 2, :], geB[:, t % 2, :], ALU.subtract).then_inc(s("masks"), 1)
                gk = bank[4][:, 0:G * LC * 20].rearrange("p (c e) -> p c e", e=20)
                dve.wait_ge(s("G"), g + 1)
                v_.tensor_tensor(rel[:, :, :], place_col[:, :, :], gk[:, :, SLOTS:SLOTS + 2], ALU.subtract).then_inc(s("decode"), 1)
                k += 1
                dve.wait_ge(s("decode"), base + k)
                v_.tensor_tensor(hit[:, :, :].rearrange("p c (h e) -> p (c h) e", h=2),
                                 rel[:, :, :].rearrange("p c h -> p (c h)").unsqueeze(2).broadcast_to([P, G * LC * 2, 8]),
                                 slot_row[:, :].unsqueeze(1).broadcast_to([P, G * LC * 2, 8]), ALU.is_equal).then_inc(s("decode"), 1)
                k += 1
                dve.wait_ge(s("decode"), base + k)
                v_.tensor_tensor(hitk[:, :, :], hit[:, :, :], gk[:, :, 0:SLOTS], ALU.mult).then_inc(s("decode"), 1)
                k += 1
                dve.wait_ge(s("decode"), base + k)
                v_.reduce_sum(keyf[:, :], hitk[:, :, :], axis=AX.X).then_inc(s("decode"), 1)
                k += 1
                dve.wait_ge(s("decode"), base + k)
                v_.tensor_scalar(keyg[:, :], keyf[:, :], CENTRE - 1.0, 0.0, ALU.add, ALU.max).then_inc(s("decode"), 1)
                k += 1
                dve.wait_ge(s("decode"), base + k)
                v_.tensor_scalar(idx_all[:, bass.ts(g, G), :].rearrange("p t c -> p (t c)"), keyg[:, :], float(N - 1), None, ALU.min).then_inc(s("idx"), 1)
                return k

            got = lists(0, first=True)
            assert got == STEPS_OF_GROUP, got
            with dve.Fori(1, NG) as g:
                lists(g)

            dve.wait_ge(s("E"), TILES)
            v_.tensor_tensor(em_all[:, :, 0], E_all[:, :, D], E_all[:, :, D + 1], ALU.max).then_inc(s("em"), 1)
            dve.wait_ge(s("em"), 1)

            def scores(t, b, first=False):
                dve.wait_ge(s("bias"), 2 * t + 2)
                dve.wait_ge(s("Sp"), t + 1)
                if not first:
                    dve.wait_ge(s("PTp"), t - 1)
                dve.sem_inc(s("passed_v"), 1)
                v_.tensor_tensor_reduce(out=S[b][:, :], in0=bank[2][:, :], in1=bias[b][:, :], scale=1.0, scalar=-3.0e38,
                                        op0=ALU.add, op1=ALU.max, accum_out=mx[b][:, 0:1]).then_inc(s("Sm"), 1)
                dve.wait_ge(s("Sm"), t + 1)
                v_.tensor_scalar(negm[b][:, :], mx[b][:, :], one(em_all[:, bass.ts(t, 1), :]), -1.0, ALU.max, ALU.mult).then_inc(s("negm"), 1)

            def p_transposed(t, b):
                dve.wait_ge(s("PTp"), t + 1)
                v_.tensor_copy(PT[b][:, :, :], bank[3][:, :].rearrange("p (c q) -> p c q", c=CHUNKS)).then_inc(s("PT"), 1)

            def epilogue(t, j):
                b = j % 2
                dve.wait_ge(s("exp"), 2 * t + 2)
                v_.reduce_sum(st[b][:, 3:4], st[b][:, 0:3], axis=AX.X).then_inc(s("ep"), 1)
                v_.tensor_copy(one(negm_all[:, bass.ts(t, 1), :]), negm[b][:, :]).then_inc(s("ep"), 1)
                dve.wait_ge(s("ep"), 5 * t + 1)
                v_.reciprocal(st[b][:, 4:5], st[b][:, 3:4]).then_inc(s("ep"), 1)
                dve.wait_ge(s("Eb"), t + 1)
                dve.wait_ge(s("Wp"), t + 1)
                v_.scalar_tensor_tensor(acc[b][:, :], Eb[b][:, :], st[b][:, 1:2], bank[5][:, 0:D], ALU.mult, ALU.add).then_inc(s("ep"), 1)
                dve.wait_ge(s("ep"), 5 * t + 4)
                v_.scalar_tensor_tensor(acc2[b][:, :], gV_b[:, :], st[b][:, 2:3], acc[b][:, :], ALU.mult, ALU.add).then_inc(s("ep"), 1)
                dve.wait_ge(s("ep"), 5 * t + 5)
                v_.scalar_tensor_tensor(acc[b][:, :], blv_b[:, :], st[b][:, 0:1], acc2[b][:, :], ALU.mult, ALU.add).then_inc(s("y"), 1)
                dve.wait_ge(s("y"), t + 1)
                dve.wait_ge(s(f"m{j % AHEAD}"), loaded("m", t, j % AHEAD, AHEAD))
                v_.scalar_tensor_tensor(acc2[b][:, :], acc[b][:, :], st[b][:, 4:5], m_row[j % AHEAD][:, :], ALU.mult, ALU.max).then_inc(s("y2"), 1)
                dve.wait_ge(s("y2"), 2 * t + 1)
                v_.tensor_tensor(y[b][:, :], acc2[b][:, :], x_cat[j % AHEAD][:, 0, :], ALU.add).then_inc(s("y2"), 1)
                dve.wait_ge(s("y2"), 2 * t + 2)
                dve.sem_inc(s("passed_v"), 1)
                v_.bn_stats(stats[b][:, :], y[b][:, :]).then_inc(s("st"), 1)
                dve.wait_ge(s("st"), 2 * t + 1)
                dve.sem_inc(s("passed_v"), 1)
                v_.bn_aggr(mv[b][:, :], stats[b][:, :]).then_inc(s("st"), 1)

            def normalise(t, b, first=False):
                dve.wait_ge(s("pw"), 2 * t + 2)
                if not first:
                    dve.wait_ge(s(f"out{b}"), 8 * (t - b))
                v_.tensor_scalar(o_t[b][:, :], y[b][:, :], mv[b][:, 0:1], rstd[b][:, :], ALU.subtract, ALU.mult).then_inc(s("norm"), 1)

            scores(0, 0, first=True)

            def step(t, j, first=False, last=0):
                b = j % 2
                p_transposed(t, b)
                if last < 3:
                    scores(t + 1, (b + 1) % 2, first=first)
                epilogue(t, j)
                if not first:
                    normalise(t - 1, (b + 1) % 2, first=(first or (isinstance(t, int) and t <= 2)))

            step(0, 0, first=True)
            for t in range(1, AHEAD):
                step(t, t)
            with dve.Fori(1, TILES // AHEAD - 1) as i:
                for j in range(AHEAD):
                    step(AHEAD * i + j, j)
            for j in range(AHEAD):
                t = TILES - AHEAD + j
                step(t, j, last=max(0, t + 4 - TILES))
            normalise(TILES - 1, 1)
            v_.reduce_max(verdict[:, 0:1], bad_all[:, :, :].rearrange("p g e -> p (g e)"), axis=AX.X).then_inc(s("verdict"), 1)
            dve.wait_ge(s("ep"), 5 * TILES)
            v_.reduce_max(verdict[:, 1:2], negm_all[:, :, 0], axis=AX.X).then_inc(s("verdict"), 1)
            dve.wait_ge(s("verdict"), 2)
            v_.tensor_scalar(verdict[:, 2:3], verdict[:, 1:2], -SURE, verdict[:, 0:1], ALU.add, ALU.max).then_inc(s("verdict"), 1)
            dve.wait_ge(s("verdict"), 3)
            v_.tensor_scalar(verdict[:, 3:4], verdict[:, 2:3], 0.0, None, ALU.is_gt).then_inc(s("verdict"), 1)
            dve.wait_ge(s("verdictp"), 1)
            v_.tensor_copy(general_i[:, :], bank[7][:, 0:1]).then_inc(s("verdict"), 1)

        @block.tensor
        def _(pe):
            t_ = nc.tensor
            pe.wait_ge(s("const"), 8)
            pe.wait_ge(s("w1"), 48)
            for i, k in enumerate(("wlq", "wlk", "wgq")):
                for d in range(H):
                    for c in range(H):
                        last = t_.transpose(bank[5 + i][:, c * D + d * P:c * D + (d + 1) * P],
                                            w[k][:, d, c * P:(c + 1) * P], ident[:, :])
                last.then_inc(s("wT"), 1)
            pe.wait_ge(s("wTc"), 2)
            for d in range(H):
                for c in range(H):
                    last = t_.matmul(bank[3][:, d * D:(d + 1) * D], wT["wlq"][:, c, d * P:(d + 1) * P],
                                     wT["wlk"][:, c, :], start=(c == 0), stop=(c == H - 1))
            last.then_inc(s("prod"), 1)
            pe.wait_ge(s("prodc"), 1)

            def starts(g):
                pe.wait_ge(s("counts"), g + 1)
                t_.matmul(bank[3][:, 0:G], before[:, :], n_row[:, :], start=True, stop=True)
                t_.matmul(bank[3][:, G:2 * G], ones[:, :], n_row[:, :], start=True, stop=True).then_inc(s("offs"), 1)

            def slots(g):
                pe.wait_ge(s("R"), g + 1)
                pe.wait_ge(s("masks"), g * G + G)
                for t in range(G):
                    for c in range(LC):
                        o = (t * LC + c) * 20
                        last = t_.matmul(bank[4][:, o:o + SLOTS + 2],
                                         one(mask_list[:, bass.ts(g * G + t, 1), c * P:(c + 1) * P]),
                                         R[:, t, :], start=True, stop=True)
                last.then_inc(s("G"), 1)

            starts(0)
            slots(0)
            pe.wait_ge(s("xsum"), 5)
            pe.wait_ge(s("w"), nW)
            for h in range(H):
                last = t_.matmul(bank[5][:, h * P:(h + 1) * P], E_all[:, 0, h * P:(h + 1) * P], mean_sq[:, :], start=True, stop=True)
            last.then_inc(s("prod"), 1)
            pe.wait_ge(s("prodc"), 2)
            for c in range(H):
                for h in range(H):
                    last = t_.matmul(bank[6][:, c:c + 1], w["wgk"][:, h, c * P:(c + 1) * P], xbarB[:, h, 0:1],
                                     start=(h == 0), stop=(h == H - 1))
            last.then_inc(s("prod"), 1)
            for h in range(H):
                t_.matmul(bank[7][:, 0:D], xbarB[:, h, :], w["wgv"][:, h, :], start=(h == 0), stop=False)
            t_.matmul(bank[7][:, 0:D], ones[0:1, :], bgv_b[0:1, :], start=False, stop=True).then_inc(s("prod"), 1)
            pe.wait_ge(s("prodc"), 3)
            for h in range(H):
                for c in range(H):
                    last = t_.matmul(bank[5][:, h:h + 1], wT["wgq"][:, c, h * P:(h + 1) * P], gKT[:, c:c + 1],
                                     start=(c == 0), stop=(c == H - 1))
            last.then_inc(s("prod"), 1)
            pe.wait_ge(s("prodc"), 5)

            def prologue(t, b, first=False):
                pe.wait_ge(s(f"mt{b}"), loaded("mt", t, b, 2))
                if not first:
                    pe.wait_ge(s("mT"), t)
                for h in range(H):
                    last = t_.transpose(bank[0][:, h * P:(h + 1) * P], m_t[b][:, h * P:(h + 1) * P], ident[:, :])
                last.then_inc(s("mTp"), 1)
                pe.wait_ge(s("mT"), t + 1)
                if not first:
                    pe.wait_ge(s("TT"), t)
                for o in range(H):
                    for h in range(H):
                        last = t_.matmul(bank[1][:, o * P:(o + 1) * P], A[:, h, o * P:(o + 1) * P], mT[b][:, h, :],
                                         start=(h == 0), stop=(h == H - 1))
                last.then_inc(s("TTp"), 1)
                if not first:
                    pe.wait_ge(s("E"), t)
                for h in range(H):
                    last = t_.matmul(bank[2][:, 0:D + 2], mT[b][:, h, :], wevx[:, h, :], start=(h == 0), stop=(h == H - 1))
                last.then_inc(s("Ep"), 1)

            for t in range(G):
                prologue(t, t % 2, first=(t == 0))
            with pe.Fori(1, NG) as g:
                starts(g)
                slots(g)
                for t in range(G):
                    prologue(g * G + t, t % 2)

            def x_transposes(t, j, first=False):
                j = j % AHEAD
                pe.wait_ge(s(f"xt{j}"), loaded("xt", t, j, AHEAD))
                pe.wait_ge(s(f"gath{j}"), loaded("gath", t, j, AHEAD, LC))
                for h in range(H):
                    if not first:
                        pe.wait_ge(s("xT"), 2 * t + h - 1)
                    for c in range(CHUNKS):
                        last = t_.transpose(bank[h][:, c * P:(c + 1) * P], x_cat[j % AHEAD][:, c, h * P:(h + 1) * P], ident[:, :])
                    last.then_inc(s("xTp"), 1)

            def scores(t, b, first=False):
                pe.wait_ge(s("TTc"), t + 1)
                pe.wait_ge(s("xT"), 2 * t + 2)
                if not first:
                    pe.wait_ge(s("Sm"), t)
                for h in range(H):
                    last = t_.matmul(bank[2][:, :], TT[b][:, h * P:(h + 1) * P], xT[b][:, h, :], start=(h == 0), stop=(h == H - 1))
                last.then_inc(s("Sp"), 1)

            pe.wait_ge(s("E"), TILES)
            pe.wait_ge(s("idx"), NG)
            x_transposes(0, 0, first=True)
            x_transposes(1, 1)
            scores(0, 0, first=True)

            def step(t, j, first=False, last=0):
                b = j % 2
                pe.wait_ge(s("exp"), 2 * t + 1)
                if not first:
                    pe.wait_ge(s("PT"), t)
                for c in range(CHUNKS):
                    ins = t_.transpose(bank[3][:, c * P:(c + 1) * P], S[b][:, c * P:(c + 1) * P], ident[:, :])
                ins.then_inc(s("PTp"), 1)
                if last < 3:
                    scores(t + 1, (b + 1) % 2)
                pe.wait_ge(s("PT"), t + 1)
                if not first:
                    pe.wait_ge(s("OT"), t)
                for h in range(H):
                    for c in range(CHUNKS):
                        ins = t_.matmul(bank[4][:, h * P:(h + 1) * P], x_cat[j % AHEAD][:, c, h * P:(h + 1) * P], PT[b][:, c, :],
                                        start=(c == 0), stop=(c == CHUNKS - 1))
                ins.then_inc(s("OTp"), 1)
                if last < 2:
                    x_transposes(t + 2, j + 2)
                pe.wait_ge(s("OT"), t + 1)
                if not first:
                    pe.wait_ge(s("y"), t)
                for h in range(H):
                    ins = t_.matmul(bank[5][:, 0:D], OT[b][:, h, :], w["wlv"][:, h, :], start=(h == 0), stop=(h == H - 1))
                ins.then_inc(s("Wp"), 1)

            step(0, 0, first=True)
            for t in range(1, AHEAD):
                step(t, t)
            with pe.Fori(1, TILES // AHEAD - 1) as i:
                for j in range(AHEAD):
                    step(AHEAD * i + j, j)
            for j in range(AHEAD):
                t = TILES - AHEAD + j
                step(t, j, last=max(0, t + 4 - TILES))
            pe.wait_ge(s("verdict"), 4)
            t_.matmul(bank[7][:, 0:1], ones[:, :], verdict[:, 3:4], start=True, stop=True).then_inc(s("verdictp"), 1)

        block_ctx.__exit__(None, None, None)

        x_all = E_all[:, :, 0:D]
        xT_all = T_all[:, :, :, :].rearrange("p t h k -> p (t h k)").rearrange("p (h n) -> p h n", h=H)
        Sg = mask_list[:, :, :].rearrange("p t n -> p (t n)").bitcast(F32)[:, 0:N]
        adj_g = adj_p[0][:, 0, :]
        Eg = or1[:, :, :].rearrange("p j n -> p (j n)").bitcast(F32)[:, 0:D + 2]
        Og = adj_p[0][:, 1, 0:4 * D].bitcast(F32)
        m_g, mT_g, TT_g, PT_g, OT_g, st_g = m_t[0], mT[0], TT[0], PT, OT[0], st[0]
        acc_g, acc2_g, y_g, o_g, mv_g, rstd_g, ve_g, stats_g = acc[0], acc2[0], y[0], o_t[0], mv[0], rstd[0], ve[0], stats[0]
        for n in ("x adj m fill mTp mT TTp TT Ep E S Sm nmax exp PTp PT PV Ox OTp OT O y pw norm out xtp xtc chain".split()):
            s("g_" + n)

        gblock = ctx.enter_context(nc.Block())

        @gblock.sync
        def _(sp):
            general = sp.value_load(general_i[0:1, 0:1], min_val=0, max_val=P)
            with sp.If(general != 0):
                for q in range(4):
                    ts = slice(q * TILES // 4, (q + 1) * TILES // 4)
                    sp.dma_start(x_all[:, ts, :], rows(x)[:, ts, :]).then_inc(s("g_x"), 16)
                sp.dma_start(adj_g, adj[0:P, :]).then_inc(s("g_adj"), 16)
                sp.dma_start(m_g[:, :], masked_x[0:P, :]).then_inc(s("g_m"), 16)
                with sp.Fori(1, TILES) as t:
                    sp.wait_ge(s("g_Sm"), t * GROUPS)
                    sp.dma_start(adj_g, adj[bass.ts(t, P), :]).then_inc(s("g_adj"), 16)
                    sp.wait_ge(s("g_norm"), t)
                    sp.dma_start(out[bass.ts(t - 1, P), :], o_g[:, :]).then_inc(s("g_out"), 16)
                    sp.wait_ge(s("g_out"), 16 * t)
                    sp.dma_start(m_g[:, :], masked_x[bass.ts(t, P), :]).then_inc(s("g_m"), 16)
                sp.wait_ge(s("g_norm"), TILES)
                sp.dma_start(out[(TILES - 1) * P:N, :], o_g[:, :]).then_inc(s("g_out"), 16)
                sp.wait_ge(s("g_out"), 16 * TILES)

        @gblock.gpsimd
        def _(pool):
            g_ = nc.gpsimd
            general = pool.value_load(general_i[0:1, 0:1], min_val=0, max_val=P)
            with pool.If(general != 0):
                g_.memset(Sg, MASKED).then_inc(s("g_fill"), 1)
                with pool.Fori(0, TILES) as t:
                    pool.wait_ge(s("g_y"), 4 * t + 4)
                    g_.tensor_tensor(ve_g[:, :], mv_g[:, 1:2], eps_col[:, :], ALU.add).then_inc(s("g_pw"), 1)
                    pool.wait_ge(s("g_pw"), 2 * t + 1)
                    g_.tensor_tensor(rstd_g[:, :], ve_g[:, :], power[:, :], ALU.pow).then_inc(s("g_pw"), 1)
                    pool.wait_ge(s("g_PTp"), t * GROUPS + GROUPS)
                    pool.sem_inc(s("passed_p"), 1)
                    g_.memset(Sg, MASKED).then_inc(s("g_fill"), 1)

        @gblock.scalar
        def _(act):
            a_ = nc.scalar
            general = act.value_load(general_i[0:1, 0:1], min_val=0, max_val=P)
            with act.If(general != 0):
                with act.Fori(0, TILES // 2) as c:
                    act.wait_ge(s("g_xtp"), c + 1)
                    a_.copy(xT_all[:, :, bass.ts(c, 2 * P)], halves(bank[6][:, :])).then_inc(s("g_xtc"), 1)
                with act.Fori(0, TILES) as t:
                    act.wait_ge(s("g_mTp"), t + 1)
                    a_.copy(mT_g[:, :, :], halves(bank[0][:, 0:D])).then_inc(s("g_mT"), 1)
                    act.wait_ge(s("g_TTp"), t + 1)
                    a_.copy(TT_g[:, :], bank[1][:, 0:D]).then_inc(s("g_TT"), 1)
                    act.wait_ge(s("g_nmax"), t + 1)
                    a_.activation(Sg, Sg, ACT.Exp, bias=st_g[:, 6:7], accum_out=st_g[:, 0:1]).then_inc(s("g_exp"), 1)
                    a_.activation(st_g[:, 1:3], Eg[:, D:D + 2], ACT.Exp, bias=st_g[:, 6:7]).then_inc(s("g_exp"), 1)
                    for g in range(1, GROUPS, 2):
                        act.wait_ge(s("g_PTp"), t * GROUPS + g + 1)
                        a_.copy(PT_g[1][:, :, :], bank[2 + g % 2][:, :].rearrange("p (c q) -> p c q", c=CHUNKS)).then_inc(s("g_PT"), 1)
                    act.wait_ge(s("g_OTp"), t + 1)
                    a_.copy(OT_g[:, :, :], halves(bank[0][:, 0:D])).then_inc(s("g_OT"), 1)

        @gblock.vector
        def _(dve):
            v_ = nc.vector
            general = dve.value_load(general_i[0:1, 0:1], min_val=0, max_val=P)
            with dve.If(general != 0):
                with dve.Fori(0, TILES) as t:
                    dve.wait_ge(s("g_Ep"), t + 1)
                    v_.tensor_copy(Eg, bank[7][:, 0:D + 2]).then_inc(s("g_E"), 1)
                    dve.wait_ge(s("g_fill"), t + 1)
                    dve.wait_ge(s("g_adj"), 16 * t + 16)
                    for g in range(GROUPS):
                        dve.wait_ge(s("g_S"), t * GROUPS + g + 1)
                        dve.sem_inc(s("passed_v"), 1)
                        v_.copy_predicated(Sg[:, g * GROUP:(g + 1) * GROUP], adj_g[:, g * GROUP:(g + 1) * GROUP],
                                           bank[4 + g % 2][:, :]).then_inc(s("g_Sm"), 1)
                    dve.wait_ge(s("g_Sm"), (t + 1) * GROUPS)
                    v_.reduce_max(st_g[:, 3:4], Sg, axis=AX.X).then_inc(s("g_chain"), 1)
                    dve.wait_ge(s("g_E"), t + 1)
                    v_.reduce_max(st_g[:, 5:6], Eg[:, D:D + 2], axis=AX.X).then_inc(s("g_chain"), 1)
                    dve.wait_ge(s("g_chain"), 8 * t + 2)
                    v_.tensor_scalar(st_g[:, 6:7], st_g[:, 3:4], st_g[:, 5:6], -1.0, ALU.max, ALU.mult).then_inc(s("g_nmax"), 1)
                    for g in range(0, GROUPS, 2):
                        dve.wait_ge(s("g_PTp"), t * GROUPS + g + 1)
                        v_.tensor_copy(PT_g[0][:, :, :], bank[2 + g % 2][:, :].rearrange("p (c q) -> p c q", c=CHUNKS)).then_inc(s("g_PT"), 1)
                    dve.wait_ge(s("g_PV"), (t + 1) * GROUPS)
                    v_.tensor_copy(Og, bank[6][:, 0:D]).then_inc(s("g_Ox"), 1)
                    dve.wait_ge(s("g_exp"), 2 * t + 2)
                    v_.reduce_sum(st_g[:, 7:8], st_g[:, 0:3], axis=AX.X).then_inc(s("g_chain"), 1)
                    dve.wait_ge(s("g_chain"), 8 * t + 3)
                    v_.reciprocal(st_g[:, 4:5], st_g[:, 7:8]).then_inc(s("g_chain"), 1)
                    v_.tensor_tensor(acc_g[:, :], Eg[:, 0:D], bev_b[:, :], ALU.add).then_inc(s("g_chain"), 1)
                    dve.wait_ge(s("g_O"), t + 1)
                    dve.wait_ge(s("g_chain"), 8 * t + 5)
                    v_.scalar_tensor_tensor(acc2_g[:, :], acc_g[:, :], st_g[:, 1:2], bank[7][:, 0:D], ALU.mult, ALU.add).then_inc(s("g_chain"), 1)
                    dve.wait_ge(s("g_chain"), 8 * t + 6)
                    v_.scalar_tensor_tensor(acc_g[:, :], gV_b[:, :], st_g[:, 2:3], acc2_g[:, :], ALU.mult, ALU.add).then_inc(s("g_chain"), 1)
                    dve.wait_ge(s("g_chain"), 8 * t + 7)
                    v_.scalar_tensor_tensor(acc2_g[:, :], blv_b[:, :], st_g[:, 0:1], acc_g[:, :], ALU.mult, ALU.add).then_inc(s("g_chain"), 1)
                    dve.wait_ge(s("g_chain"), 8 * t + 8)
                    dve.wait_ge(s("g_m"), 16 * t + 16)
                    v_.scalar_tensor_tensor(acc_g[:, :], acc2_g[:, :], st_g[:, 4:5], m_g[:, :], ALU.mult, ALU.max).then_inc(s("g_y"), 1)
                    dve.wait_ge(s("g_y"), 4 * t + 1)
                    v_.tensor_tensor(y_g[:, :], acc_g[:, :], one(x_all[:, bass.ts(t, 1), :]), ALU.add).then_inc(s("g_y"), 1)
                    dve.wait_ge(s("g_y"), 4 * t + 2)
                    dve.sem_inc(s("passed_v"), 1)
                    v_.bn_stats(stats_g[:, :], y_g[:, :]).then_inc(s("g_y"), 1)
                    dve.wait_ge(s("g_y"), 4 * t + 3)
                    dve.sem_inc(s("passed_v"), 1)
                    v_.bn_aggr(mv_g[:, :], stats_g[:, :]).then_inc(s("g_y"), 1)
                    dve.wait_ge(s("g_pw"), 2 * t + 2)
                    v_.tensor_scalar(o_g[:, :], y_g[:, :], mv_g[:, 0:1], rstd_g[:, :], ALU.subtract, ALU.mult).then_inc(s("g_norm"), 1)

        @gblock.tensor
        def _(pe):
            t_ = nc.tensor
            general = pe.value_load(general_i[0:1, 0:1], min_val=0, max_val=P)
            with pe.If(general != 0):
                pe.wait_ge(s("g_x"), 64)
                for c in range(TILES // 2):
                    if c >= 1:
                        pe.wait_ge(s("g_xtc"), c)
                    for j in range(2):
                        for h in range(H):
                            last = t_.transpose(bank[6][:, h * 2 * P + j * P:h * 2 * P + (j + 1) * P],
                                                E_all[:, 2 * c + j, h * P:(h + 1) * P], ident[:, :])
                    last.then_inc(s("g_xtp"), 1)
                pe.wait_ge(s("g_xtc"), TILES // 2)
                with pe.Fori(0, TILES) as t:
                    pe.wait_ge(s("g_m"), 16 * t + 16)
                    for h in range(H):
                        last = t_.transpose(bank[0][:, h * P:(h + 1) * P], m_g[:, h * P:(h + 1) * P], ident[:, :])
                    last.then_inc(s("g_mTp"), 1)
                    pe.wait_ge(s("g_mT"), t + 1)
                    for o in range(H):
                        for h in range(H):
                            last = t_.matmul(bank[1][:, o * P:(o + 1) * P], A[:, h, o * P:(o + 1) * P], mT_g[:, h, :],
                                             start=(h == 0), stop=(h == H - 1))
                    last.then_inc(s("g_TTp"), 1)
                    for h in range(H):
                        last = t_.matmul(bank[7][:, 0:D + 2], mT_g[:, h, :], wevx[:, h, :], start=(h == 0), stop=(h == H - 1))
                    last.then_inc(s("g_Ep"), 1)
                    pe.wait_ge(s("g_TT"), t + 1)
                    for g in range(GROUPS):
                        if g >= 2:
                            pe.wait_ge(s("g_Sm"), t * GROUPS + g - 1)
                        for h in range(H):
                            last = t_.matmul(bank[4 + g % 2][:, :], TT_g[:, h * P:(h + 1) * P], xT_all[:, h, g * GROUP:(g + 1) * GROUP],
                                             start=(h == 0), stop=(h == H - 1))
                        last.then_inc(s("g_S"), 1)

                    def transposes(g):
                        if g >= 2:
                            pe.wait_ge(s("g_PT"), t * GROUPS + g - 1)
                        for c in range(CHUNKS):
                            k = g * GROUP + c * P
                            last = t_.transpose(bank[2 + g % 2][:, c * P:(c + 1) * P], Sg[:, k:k + P], ident[:, :])
                        last.then_inc(s("g_PTp"), 1)

                    def products(g):
                        pe.wait_ge(s("g_PT"), t * GROUPS + g + 1)
                        for c in range(CHUNKS):
                            last = t_.matmul(bank[6][:, 0:D], PT_g[g % 2][:, c, :], E_all[:, g * CHUNKS + c, 0:D],
                                             start=(g == 0 and c == 0), stop=(g == GROUPS - 1 and c == CHUNKS - 1))
                        last.then_inc(s("g_PV"), 1)

                    pe.wait_ge(s("g_exp"), 2 * t + 1)
                    transposes(0)
                    for g in range(GROUPS):
                        products(g)
                        if g + 1 < GROUPS:
                            transposes(g + 1)
                    pe.wait_ge(s("g_Ox"), t + 1)
                    for h in range(H):
                        last = t_.transpose(bank[0][:, h * P:(h + 1) * P], Og[:, h * P:(h + 1) * P], ident[:, :])
                    last.then_inc(s("g_OTp"), 1)
                    pe.wait_ge(s("g_OT"), t + 1)
                    for h in range(H):
                        last = t_.matmul(bank[7][:, 0:D], OT_g[:, h, :], w["wlv"][:, h, :], start=(h == 0), stop=(h == H - 1))
                    last.then_inc(s("g_O"), 1)


_INS = ["x", "adj", "L0_gnn_masked_x", "L0_gnn_Wlq", "L0_gnn_Wlk", "L0_gnn_Wlv", "L0_gnn_blv", "L0_gnn_Wgq",
        "L0_gnn_Wgk", "L0_gnn_Wgv", "L0_gnn_bgv", "L0_gnn_Wes", "L0_gnn_Wev", "L0_gnn_bev"]


def kernel(**inputs):
    import concourse.bacc as bacc
    from concourse.bass_utils import run_bass_kernel_spmd

    nc = bacc.Bacc("TRN2", target_bir_lowering=False, num_devices=1)
    arrays, args = {}, []
    for name in _INS:
        a = np.ascontiguousarray(inputs[name])
        arrays[f"in_{name}"] = a
        args.append(nc.dram_tensor(f"in_{name}", a.shape, mybir.dt.from_np(a.dtype), kind="ExternalInput").ap())
    args.append(nc.dram_tensor("out_rows", (N, D), F32, kind="ExternalOutput").ap())
    build(nc, *args)
    r = run_bass_kernel_spmd(nc, [arrays], core_ids=[0])
    return r.results[0]["out_rows"]
```

```python
import numpy as np
import concourse.bass as bass
from concourse import mybir
from contextlib import ExitStack

F32 = mybir.dt.float32
F16 = mybir.dt.float16
I32 = mybir.dt.int32
U32 = mybir.dt.uint32
U16 = mybir.dt.uint16
U8 = mybir.dt.uint8
ALU = mybir.AluOpType
ACT = mybir.ActivationFunctionType
AX = mybir.AxisListType

N = 4096
D = 256
P = 128
H = D // P
TILES = N // P
GROUP = 512
GROUPS = N // GROUP
CHUNKS = GROUP // P
MASKED = -1000000000.0
UNLISTED = -1.0e30
SURE = 9.0e8
SCALE = 1.0 / 16.0
EPS = 1e-05

G = 8
NG = TILES // G
PAIRS = TILES // 2
WORDS = 256
SLOTS = 16
LEVELS = 2
LISTED = 320
LC = -(-LISTED // P)
FILL = [min(P, LISTED - c * P) for c in range(LC)]
KEYS = P + LISTED
CENTRE = 2048.0
EXPONENT = 0x7F800000
STEPS_OF_GROUP = 53
AHEAD = 4
EARLY = 6
ROWS = 8


def build(nc, x, adj, masked_x, Wlq, Wlk, Wlv, blv, Wgq, Wgk, Wgv, bgv, Wes, Wev, bev, out):
    ctx = ExitStack()
    with ctx:
        def sb(name, shape, dt=F32):
            return ctx.enter_context(nc.sbuf_tensor(name, shape, dt))

        def sem(name):
            return ctx.enter_context(nc.semaphore(name))

        half = lambda a: a.rearrange("(h p) n -> p h n", p=P)
        rows = lambda a: a.rearrange("(t p) d -> p t d", p=P)
        halves = lambda a: a.rearrange("p (h k) -> p h k", h=H)
        one = lambda a: a.rearrange("p a d -> p (a d)")

        x_all = sb("x_all", [P, TILES, D])
        area = sb("area", [P, H, N])
        mask_own = [sb(f"mask_own{i}", [P, P], U8) for i in range(ROWS)]
        mask_list = sb("mask_list", [P, G, LISTED], F16)
        Sg = sb("Sg", [P, N])
        idx_all = sb("idx_all", [P, TILES, LC], U32)
        negm_all = sb("negm_all", [P, TILES, 1])
        bad_all = sb("bad_all", [P, NG, 3])
        w = {k: sb(k, [P, H, D]) for k in ("wlq", "wlk", "wlv", "wgq", "wgk", "wgv")}
        xT = [sb(f"xT{i}", [P, H, GROUP]) for i in range(2)]
        wT = {k: halves(v) for k, v in (("wlq", xT[0][:, 0, :]), ("wlk", xT[0][:, 1, :]), ("wgq", xT[1][:, 0, :]))}
        A = sb("A", [P, H, D])
        wevx = sb("wevx", [P, H, D + 2])
        blv_b = sb("blv_b", [P, D])
        bev_b = sb("bev_b", [P, D])
        bgv_b = sb("bgv_b", [P, D])
        gV_b = sb("gV_b", [P, D])
        ident = sb("ident", [P, P])
        verdict = sb("verdict", [P, 4])
        general_i = sb("general_i", [P, 1], I32)
        before = sb("before", [P, P])
        ones = sb("ones", [P, P])
        mean_col = sb("mean_col", [P, 1])
        eps_col = sb("eps_col", [P, 1])
        power = sb("power", [P, 1])
        word_row = sb("word_row", [P, WORDS])
        place_row = sb("place_row", [P, LISTED], F16)
        place_col = sb("place_col", [P, G * LC, 2])
        slot_row = sb("slot_row", [P, SLOTS // 2])
        zero_blk = sb("zero_blk", [P, P // 4], U32)
        xbarB = sb("xbarB", [P, H, P])
        gKT = sb("gKT", [P, H])
        adj_p = [sb(f"adj_p{i}", [P, 2, N], U8) for i in range(2)]
        or1 = sb("or1", [P, 2, 512], U32)
        or2 = sb("or2", [P, 2, 256], U32)
        or3 = sb("or3", [P, 2, 128], U32)
        code = sb("code", [P, 2, WORDS])
        top = sb("top", [P, G, SLOTS])
        topi = sb("topi", [P, G * SLOTS], I32)
        place2 = sb("place2", [P, G * SLOTS], I32)
        word_i = sb("word_i", [P, G * SLOTS], I32)
        bits = sb("bits", [P, LEVELS + 1, G * SLOTS])
        high = sb("high", [P, LEVELS, G * SLOTS], I32)
        kx = sb("kx", [P, LEVELS, G * SLOTS], I32)
        ku = sb("ku", [P, LEVELS, G * SLOTS], I32)
        kv = sb("kv", [P, LEVELS, G * SLOTS])
        cand = sb("cand", [P, LEVELS, G * SLOTS])
        keys1 = sb("keys1", [P, G, SLOTS])
        some = sb("some", [P, G, SLOTS])
        n2 = sb("n2", [P, G, 2])
        n_row = sb("n_row", [P, G])
        off = sb("off", [P, G])
        end = sb("end", [P, G])
        mxt = sb("mxt", [P, G])
        R = sb("R", [P, G, SLOTS + 2], F16)
        near = sb("near", [P, G, LISTED], F16)
        rel = sb("rel", [P, G * LC, 2])
        hit = sb("hit", [P, G * LC, SLOTS])
        hitk = sb("hitk", [P, G * LC, SLOTS])
        keyf = sb("keyf", [P, G * LC])
        keyg = sb("keyg", [P, G * LC])
        carve = area[:, :, :].rearrange("p h n -> p (h n)")
        m_row = [carve[:, i * D:(i + 1) * D] for i in range(ROWS)]
        x_own = [carve[:, (ROWS + i) * D:(ROWS + i + 1) * D] for i in range(ROWS)]
        x_list = [carve[:, (2 * ROWS + LC * i) * D:(2 * ROWS + LC * (i + 1)) * D].rearrange("p (c d) -> p c d", c=LC)
                  for i in range(AHEAD)]
        adj_first = [carve[:, (2 * ROWS + 8 * i) * D:(2 * ROWS + 8 * (i + 1)) * D].bitcast(U8).rearrange("p (j n) -> p j n", j=2)
                     for i in range(2)]
        TT_early = [sb(f"TT_early{i}", [P, D]) for i in range(EARLY - 1)]
        E_early = [x_all[:, 2 * i:2 * i + 2, :].rearrange("p t d -> p (t d)")[:, 0:D + 2] for i in range(EARLY - 3)]
        mT = sb("mT", [P, H, P])
        TT = [sb(f"TT{i}", [P, H * P]) for i in range(2)]
        idx_t = [sb(f"idx_t{i}", [P, LC], U32) for i in range(AHEAD)]
        E = [sb(f"E{i}", [P, D + 2]) for i in range(AHEAD)]
        em = [sb(f"em{i}", [P, 1]) for i in range(2)]
        bias = [x_all[:, 2 * EARLY + 6 + 2 * i:2 * EARLY + 8 + 2 * i, :].rearrange("p t d -> p (t d)") for i in range(AHEAD)]
        S = [sb(f"S{i}", [P, GROUP]) for i in range(2)]
        PT = [sb(f"PT{i}", [P, CHUNKS, P]) for i in range(2)]
        parts = [[x_all[:, 2 * EARLY + 3 * i + n, :] for n in range(3)] for i in range(2)]
        OT = [sb(f"OT{i}", [P, H, P]) for i in range(2)]
        mT_early = [halves(Sg[:, i * D:(i + 1) * D]) for i in range(EARLY)]
        mx = [sb(f"mx{i}", [P, 1]) for i in range(2)]
        negm = [sb(f"negm{i}", [P, 1]) for i in range(AHEAD)]
        st = [sb(f"st{i}", [P, 8]) for i in range(AHEAD)]
        acc = [sb(f"acc{i}", [P, D]) for i in range(2)]
        acc2 = [sb(f"acc2{i}", [P, D]) for i in range(2)]
        y = [sb(f"y{i}", [P, D]) for i in range(2)]
        o_t = [sb(f"o_t{i}", [P, D]) for i in range(2)]
        stats = [sb(f"stats{i}", [P, 6]) for i in range(2)]
        mv = [sb(f"mv{i}", [P, 2]) for i in range(2)]
        ve = [sb(f"ve{i}", [P, 1]) for i in range(2)]
        rstd = [sb(f"rstd{i}", [P, 1]) for i in range(2)]

        bank = [ctx.enter_context(nc.psum_tensor(f"bank{i}", [P, 512], F32)) for i in range(8)]

        S_ = {}

        def s(name):
            if name not in S_:
                S_[name] = sem("s_" + name)
            return S_[name]

        for n in ("w w1 x const gconst zeroed or1 or2 or3 code top decode counts offs R masks G idx "
                  "wT wTc prod prodc xsum xsum_v passed_v passed_p mTp mT TTp TT Ep E em part parts Eb "
                  "idxc bias xTp xT Sp Sm negm exp PTp PT OTp OT Wp ep acc y st pw norm verdict verdictp").split():
            s(n)

        nW = 8 * 16

        def loaded(name, t, buf, of, dmas=1):
            return 16 * dmas // of * (t - buf) + 16 * dmas

        for i in range(2):
            s(f"out{i}")
        for i in range(4):
            s(f"adj{i}")
            s(f"x{i}")
        for i in range(AHEAD):
            s(f"gath{i}")
        for i in range(ROWS):
            s(f"m{i}")
            s(f"own{i}")

        LEAD = 4
        LAG = 2

        def TT_of(t, k):
            return TT_early[t] if isinstance(t, int) and t < EARLY - 1 else TT[k % 2]

        def E_of(t, k):
            return E_early[t] if isinstance(t, int) and t < EARLY - 3 else E[k % AHEAD]

        def values_of(t):
            if isinstance(t, int) and t < EARLY - 2:
                return [t + 3] if 0 < t + 3 < EARLY else []
            return [t + 2] if tile(t + 2) else []

        def early(t):
            return isinstance(t, int) and t < EARLY

        def tile(t):
            return not isinstance(t, int) or 0 <= t < TILES

        def listed(g):
            return not isinstance(g, int) or g < NG

        def some_wait(n):
            return not isinstance(n, int) or n > 0

        def schedule(eng, step):
            for j in range(G):
                step(0, j - LEAD, j, (j + G - LEAD) % G)
            with eng.Fori(1, NG - 1) as g:
                for j in range(G):
                    step(g, G * g + (j - LEAD), j, (j + G - LEAD) % G)
            for j in range(G + LEAD + LAG):
                step(NG - 1, G * (NG - 1) - LEAD + j, j, (j + G - LEAD) % G)

        block_ctx = nc.Block()
        block = block_ctx.__enter__()

        @block.sync
        def _(sp):
            def load_pair(p, buf):
                sp.dma_start((adj_p + adj_first)[buf][:, :, :], adj[bass.ts(p, 2 * P), :].rearrange("(j p) n -> p j n", p=P)).then_inc(s(f"adj{buf}"), 16)

            def masked_in(t, r):
                sp.dma_start(m_row[r], masked_x[bass.ts(t, P), :]).then_inc(s(f"m{r}"), 16)

            def own_in(t, r):
                sp.dma_start(x_own[r], x[bass.ts(t, P), :]).then_inc(s(f"own{r}"), 16)
                sp.dma_start(mask_own[r][:, :], adj[bass.ts(t, P), bass.ts(t, P)]).then_inc(s(f"own{r}"), 16)

            load_pair(0, 0)
            for name, a in (("wlq", Wlq), ("wlk", Wlk), ("wgq", Wgq)):
                sp.dma_start(w[name][:, :, :], half(a)).then_inc(s("w1"), 16)
            load_pair(1, 1)
            load_pair(2, 2)
            for t in range(EARLY):
                masked_in(t, t)
            load_pair(3, 3)
            for q in range(4):
                ts = slice(q * TILES // 4, (q + 1) * TILES // 4)
                sp.dma_start(x_all[:, ts, :], rows(x)[:, ts, :]).then_inc(s(f"x{q}"), 16)
            for t in range(EARLY):
                own_in(t, t)
            for name, a in (("wlv", Wlv), ("wgk", Wgk), ("wgv", Wgv)):
                sp.dma_start(w[name][:, :, :], half(a)).then_inc(s("w"), 16)
            sp.dma_start(wevx[:, :, 0:D], half(Wev)).then_inc(s("w"), 16)
            sp.dma_start(wevx[:, :, D + 1:D + 2], half(Wes), allow_slow_non_contiguous=True).then_inc(s("w"), 16)
            for b, a in ((blv_b, blv), (bev_b, bev), (bgv_b, bgv)):
                sp.dma_start(b[:, 0:D], a.rearrange("(a n) -> a n", a=1).broadcast_to([P, D])).then_inc(s("w"), 16)

            def step(g, t, j, k):
                if tile(t + 5) and not early(t + 5):
                    if some_wait(t - 2):
                        sp.wait_ge(s("norm"), t - 2)
                    masked_in(t + 5, (k + 5) % ROWS)
                    own_in(t + 5, (k + 5) % ROWS)
                first = (g + 1) * (G // 2)
                if listed(g + 1) and j == 0:
                    sp.wait_ge(s("or1"), first)
                    load_pair(first, 0)
                    load_pair(first + 1, 1)
                elif listed(g + 1) and j < G // 2 - 1:
                    sp.wait_ge(s("or1"), first + j)
                    load_pair(first + j + 1, (j + 1) % 2)
                if tile(t - 2):
                    sp.wait_ge(s("norm"), t - 1)
                    sp.dma_start(out[bass.ts(t - 2, P), :], o_t[k % 2][:, :]).then_inc(s(f"out{k % 2}"), 16)

            schedule(sp, step)
            for b in range(2):
                sp.wait_ge(s(f"out{b}"), 8 * TILES)

        @block.gpsimd
        def _(pool):
            g_ = nc.gpsimd
            g_.memset(ident[:, :], 0.0).then_inc(s("gconst"), 1)
            g_.memset(ones[:, :], 1.0).then_inc(s("gconst"), 1)
            g_.memset(zero_blk[:, :], 0).then_inc(s("gconst"), 1)
            g_.iota(word_row[:, :], [[1, WORDS]], base=0, channel_multiplier=0, allow_small_or_imprecise_dtypes=True).then_inc(s("gconst"), 1)
            pool.wait_ge(s("gconst"), 4)

            def without_own_blocks(p, buf, first=False):
                pool.wait_ge(s(f"adj{buf}"), 16 if first else loaded("adj", p - 2, buf, 2))
                pool.sem_inc(s("passed_p"), 1)
                for j in range(2):
                    g_.tensor_copy((adj_p + adj_first)[buf][:, j, :].bitcast(U32)[:, bass.ts(2 * p + j, P // 4)], zero_blk[:, :]).then_inc(s("zeroed"), 1)

            without_own_blocks(0, 0, first=True)
            g_.affine_select(out=ident[:, :], in_=ident[:, :], compare_op=ALU.not_equal, fill=1.0,
                             base=0, pattern=[[-1, P]], channel_multiplier=1).then_inc(s("const"), 1)
            g_.affine_select(out=before[:, :], in_=ones[:, :], compare_op=ALU.is_gt, fill=0.0,
                             base=0, pattern=[[1, P]], channel_multiplier=-1).then_inc(s("const"), 1)
            g_.memset(mean_col[:, :], 1.0 / N).then_inc(s("const"), 1)
            g_.memset(eps_col[:, :], EPS).then_inc(s("const"), 1)
            g_.memset(power[:, :], -0.5).then_inc(s("const"), 1)
            g_.iota(place_row[:, :], [[1, LISTED]], base=0, channel_multiplier=0, allow_small_or_imprecise_dtypes=True).then_inc(s("const"), 1)
            g_.iota(place_col[:, :, :], [[0, G], [P, LC], [0, 2]], base=0, channel_multiplier=1, allow_small_or_imprecise_dtypes=True).then_inc(s("const"), 1)
            g_.iota(slot_row[:, :], [[1, SLOTS // 2]], base=0, channel_multiplier=0, allow_small_or_imprecise_dtypes=True).then_inc(s("const"), 1)
            for p in range(1, G // 2):
                without_own_blocks(p, p, first=True)
            for i in range(2):
                pool.wait_ge(s(f"x{2 * i}"), 16)
                pool.wait_ge(s(f"x{2 * i + 1}"), 16)
                for o in (16 * i, 16 * i + 4):
                    g_.tensor_tensor(x_all[:, o:o + 4, :], x_all[:, o:o + 4, :], x_all[:, o + 8:o + 12, :], ALU.add).then_inc(s("xsum"), 1)

            def step(g, t, j, k):
                if tile(t + 1):
                    Et = E_of(t + 1, k + 1)
                    pool.wait_ge(s("E"), t + 2)
                    g_.tensor_tensor(Et[:, 0:D], Et[:, 0:D], bev_b[:, :], ALU.add).then_inc(s("Eb"), 1)
                if tile(t + 3):
                    r = (k + 3) % AHEAD
                    if j:
                        pool.wait_ge(s("idx"), g + 1)
                    if some_wait(t):
                        pool.wait_ge(s("OTp"), t)
                    pool.sem_inc(s("passed_p"), 1)
                    g_.tensor_copy(idx_t[r][:, :], one(idx_all[:, bass.ts(t + 3, 1), :])).then_inc(s("idxc"), 1)
                    pool.wait_ge(s("idxc"), t + 4)
                    pool.sem_inc(s("passed_p"), 1)
                    for c in range(LC):
                        g_.indirect_dma_start(out=x_list[r][0:FILL[c], c, :], out_offset=None, in_=x,
                                              in_offset=bass.IndirectOffsetOnAxis(ap=idx_t[r][0:FILL[c], c:c + 1], axis=0),
                                              bounds_check=N - 1).then_inc(s(f"gath{r}"), 16)
                if tile(t):
                    b = k % 2
                    pool.wait_ge(s("part"), 3 * t + 2)
                    g_.tensor_tensor(parts[b][0], parts[b][0], parts[b][1], ALU.add).then_inc(s("parts"), 1)
                    pool.wait_ge(s("parts"), 2 * t + 1)
                    pool.wait_ge(s("part"), 3 * t + 3)
                    g_.tensor_tensor(parts[b][0], parts[b][0], parts[b][2], ALU.add).then_inc(s("parts"), 1)
                if tile(t - 1):
                    b = (k + 1) % 2
                    pool.wait_ge(s("st"), 2 * t)
                    g_.tensor_tensor(ve[b][:, :], mv[b][:, 1:2], eps_col[:, :], ALU.add).then_inc(s("pw"), 1)
                    pool.wait_ge(s("pw"), 2 * t - 1)
                    g_.tensor_tensor(rstd[b][:, :], ve[b][:, :], power[:, :], ALU.pow).then_inc(s("pw"), 1)
                if listed(g + 1) and j < G // 2:
                    without_own_blocks((g + 1) * (G // 2) + j, j % 2)

            schedule(pool, step)

        @block.scalar
        def _(act):
            a_ = nc.scalar

            for i, k in enumerate(("wlq", "wlk", "wgq")):
                act.wait_ge(s("wT"), i + 1)
                a_.copy(wT[k][:, :, :], halves(bank[5 + i][:, :])).then_inc(s("wTc"), 1)
            act.wait_ge(s("prod"), 1)
            a_.mul(A[:, :, :], halves(bank[3][:, :]), SCALE).then_inc(s("prodc"), 1)
            for t in range(EARLY):
                act.wait_ge(s("mTp"), t + 1)
                a_.copy(mT_early[t], halves(bank[6][:, 0:H * P])).then_inc(s("mT"), 1)
                act.wait_ge(s("TTp"), t + 1)
                a_.copy(TT_of(t, t)[:, :], bank[6][:, 0:H * P]).then_inc(s("TT"), 1)
            act.wait_ge(s("prod"), 2)
            for h in range(H):
                a_.copy(xbarB[:, h, :], bank[1 + h][:, 0:1].broadcast_to([P, P])).then_inc(s("prodc"), 1)
            act.wait_ge(s("prod"), 3)
            a_.copy(gKT[:, :], bank[3][:, 0:H]).then_inc(s("prodc"), 1)
            act.wait_ge(s("prod"), 4)
            act.wait_ge(s("w"), nW)
            a_.mul(wevx[:, :, D], bank[4][:, 0:H], SCALE).then_inc(s("prodc"), 1)

            act.wait_ge(s("Ep"), 1)
            a_.copy(E_of(0, 0)[:, :], bank[6][:, 0:D + 2]).then_inc(s("E"), 1)
            act.wait_ge(s("prod"), 5)
            a_.copy(gV_b[:, :], bank[0][:, 0:D]).then_inc(s("prodc"), 1)

            def step(g, t, j, k):
                if tile(t):
                    act.wait_ge(s("PTp"), t + 1)
                    a_.copy(PT[k % 2][:, :, :], bank[3][:, :].rearrange("p (c q) -> p c q", c=CHUNKS)).then_inc(s("PT"), 1)
                if tile(t + 4):
                    r = k % AHEAD
                    if j == 0:
                        act.wait_ge(s("masks"), g + 1)
                    if some_wait(t + 1):
                        act.wait_ge(s("Sm"), t + 1)
                    act.wait_ge(s(f"own{(k + 4) % ROWS}"), loaded("own", t + 4, (k + 4) % ROWS, ROWS, 2))
                    a_.activation(bias[r][:, 0:P], mask_own[(k + 4) % ROWS][:, :], ACT.Copy, scale=-UNLISTED, bias=UNLISTED).then_inc(s("bias"), 1)
                    a_.activation(bias[r][:, P:KEYS], mask_list[:, (k + 4) % G, :], ACT.Copy, scale=-UNLISTED, bias=UNLISTED).then_inc(s("bias"), 1)
                if tile(t + 2) and not early(t + 2):
                    act.wait_ge(s("mTp"), t + 3)
                    a_.copy(mT[:, :, :], halves(bank[6][:, 0:H * P])).then_inc(s("mT"), 1)
                if tile(t + 1):
                    r = (k + 1) % AHEAD
                    b = (k + 1) % 2
                    act.wait_ge(s("negm"), t + 2)
                    a_.activation(S[b][:, 0:KEYS], S[b][:, 0:KEYS], ACT.Exp, bias=negm[r][:, 0:1], accum_out=st[r][:, 2:3]).then_inc(s("exp"), 1)
                    a_.activation(st[r][:, 0:2], E_of(t + 1, k + 1)[:, D:D + 2], ACT.Exp, bias=negm[r][:, 0:1]).then_inc(s("exp"), 1)
                if tile(t + 2):
                    b = k % 2
                    for h in range(H):
                        act.wait_ge(s("xTp"), 2 * (t + 2) + h + 1)
                        a_.copy(xT[b][:, h, 0:KEYS], bank[h][:, 0:KEYS]).then_inc(s("xT"), 1)
                if tile(t + 2) and not early(t + 2):
                    b = k % 2
                    act.wait_ge(s("TTp"), t + 3)
                    a_.copy(TT[b][:, :], bank[6][:, 0:H * P]).then_inc(s("TT"), 1)
                if tile(t):
                    b = k % 2
                    act.wait_ge(s("OTp"), t + 1)
                    a_.copy(OT[b][:, :, :], halves(bank[4][:, 0:H * P])).then_inc(s("OT"), 1)
                for v in values_of(t):
                    act.wait_ge(s("Ep"), v + 1)
                    if not early(v):
                        act.wait_ge(s("acc"), v - 3)
                    a_.copy(E_of(v, v if isinstance(v, int) else k + 2)[:, :], bank[6][:, 0:D + 2]).then_inc(s("E"), 1)
                if tile(t + 1):
                    r = (k + 1) % AHEAD
                    b = (k + 1) % 2
                    act.wait_ge(s("exp"), 2 * t + 4)
                    if some_wait(t):
                        act.wait_ge(s("acc"), t)
                    a_.mul(parts[b][0], blv_b[:, :], st[r][:, 2:3]).then_inc(s("part"), 1)
                    a_.mul(parts[b][1], gV_b[:, :], st[r][:, 0:1]).then_inc(s("part"), 1)
                    act.wait_ge(s("Eb"), t + 2)
                    a_.mul(parts[b][2], E_of(t + 1, k + 1)[:, 0:D], st[r][:, 1:2]).then_inc(s("part"), 1)

            schedule(act, step)

        @block.vector
        def _(dve):
            v_ = nc.vector

            def pack(g, i):
                p = g * (G // 2) + i
                a = (adj_first[i - 2] if isinstance(g, int) and g == 0 and i >= 2 else adj_p[i % 2])[:, :, :].bitcast(U32)
                dve.wait_ge(s("zeroed"), 2 * p + 2)
                v_.scalar_tensor_tensor(or1[:, :, :], a[:, :, 512:1024], 4, a[:, :, 0:512],
                                        ALU.logical_shift_left, ALU.bitwise_or).then_inc(s("or1"), 1)
                dve.wait_ge(s("or1"), p + 1)
                v_.scalar_tensor_tensor(or2[:, :, :], or1[:, :, 256:512], 2, or1[:, :, 0:256],
                                        ALU.logical_shift_left, ALU.bitwise_or).then_inc(s("or2"), 1)
                dve.wait_ge(s("or2"), p + 1)
                v_.scalar_tensor_tensor(or3[:, :, :], or2[:, :, 128:256], 1, or2[:, :, 0:128],
                                        ALU.logical_shift_left, ALU.bitwise_or).then_inc(s("or3"), 1)
                dve.wait_ge(s("or3"), p + 1)
                v_.scalar_tensor_tensor(code[:, :, :], or3[:, :, :].bitcast(U16), 256.0,
                                        word_row[:, :].unsqueeze(1).broadcast_to([P, 2, WORDS]),
                                        ALU.mult, ALU.add).then_inc(s("code"), 1)
                dve.wait_ge(s("code"), p + 1)
                dve.sem_inc(s("passed_v"), 1)
                for j in range(2):
                    for h in range(2):
                        v_.max(top[:, 2 * i + j, h * 8:h * 8 + 8], code[:, j, h * P:(h + 1) * P]).then_inc(s("top"), 1)

            flat = lambda a: a.rearrange("p t s -> p (t s)")

            def decode(g):
                base = g * STEPS_OF_GROUP
                dve.wait_ge(s("top"), (g + 1) * 2 * G)
                v_.tensor_copy(topi[:, :], flat(top[:, :, :])).then_inc(s("decode"), 1)
                dve.wait_ge(s("decode"), base + 1)
                v_.tensor_scalar(word_i[:, :], topi[:, :], 8, None, ALU.logical_shift_right).then_inc(s("decode"), 1)
                v_.tensor_scalar(place2[:, :], topi[:, :], 255, 1, ALU.bitwise_and, ALU.logical_shift_left).then_inc(s("decode"), 1)
                dve.wait_ge(s("decode"), base + 2)
                v_.tensor_scalar(bits[:, 0, :], word_i[:, :], 2.0, None, ALU.mult).then_inc(s("decode"), 1)
                for l in range(LEVELS):
                    dve.wait_ge(s("decode"), base + 4 + 2 * l)
                    v_.tensor_scalar(high[:, l, :], bits[:, l, :].bitcast(I32), EXPONENT, None, ALU.bitwise_and).then_inc(s("decode"), 1)
                    dve.wait_ge(s("decode"), base + 5 + 2 * l)
                    v_.tensor_tensor(bits[:, l + 1, :], bits[:, l, :], high[:, l, :].bitcast(F32), ALU.subtract).then_inc(s("decode"), 1)
                k = 4 + 2 * LEVELS
                dve.wait_ge(s("decode"), base + k)
                raw = bits[:, 0:LEVELS, :].bitcast(I32)
                v_.tensor_scalar(kx[:, :, :], raw, 14, 0xE00, ALU.logical_shift_right, ALU.bitwise_and).then_inc(s("decode"), 1)
                v_.tensor_scalar(ku[:, :, :], raw, 26, 1, ALU.logical_shift_right, ALU.bitwise_and).then_inc(s("decode"), 1)
                v_.tensor_scalar(kv[:, :, :], bits[:, 0:LEVELS, :], 1.0, None, ALU.min).then_inc(s("decode"), 1)
                dve.wait_ge(s("decode"), base + k + 2)
                v_.tensor_tensor(high[:, :, :], kx[:, :, :], ku[:, :, :], ALU.bitwise_or).then_inc(s("decode"), 1)
                dve.wait_ge(s("decode"), base + k + 4)
                v_.tensor_tensor(kx[:, :, :], high[:, :, :], place2[:, :].unsqueeze(1).broadcast_to([P, LEVELS, G * SLOTS]), ALU.bitwise_or).then_inc(s("decode"), 1)
                dve.wait_ge(s("decode"), base + k + 5)
                v_.scalar_tensor_tensor(cand[:, :, :], kx[:, :, :], 1.0, kv[:, :, :], ALU.add, ALU.mult).then_inc(s("decode"), 1)

            def compact(g):
                base, k = g * STEPS_OF_GROUP, 14
                dve.wait_ge(s("decode"), base + k)
                dve.sem_inc(s("passed_v"), 1)
                for t in range(G):
                    for h in range(2):
                        c0 = t * SLOTS + h * 8
                        v_.max(keys1[:, t, h * 8:h * 8 + 8], cand[:, :, c0:c0 + 8]).then_inc(s("decode"), 1)
                k += 2 * G
                dve.wait_ge(s("decode"), base + k)
                v_.tensor_scalar(some[:, :, :], keys1[:, :, :], 1.0, None, ALU.min).then_inc(s("decode"), 1)
                v_.reduce_max(one(bad_all[:, bass.ts(g, 1), 0:1]), keys1[:, :, :].rearrange("p t (h e) -> p (t h) e", h=2)[:, :, 7:8].rearrange("p a b -> p (a b)"), axis=AX.X).then_inc(s("decode"), 1)
                v_.reduce_max(one(bad_all[:, bass.ts(g, 1), 1:2]), bits[:, LEVELS, :], axis=AX.X).then_inc(s("decode"), 1)
                dve.wait_ge(s("decode"), base + k + 1)
                v_.reduce_sum(n2[:, :, :].rearrange("p t h -> p (t h)"), some[:, :, :].rearrange("p t (h e) -> p (t h) e", h=2), axis=AX.X).then_inc(s("decode"), 1)
                dve.wait_ge(s("decode"), base + k + 4)
                v_.tensor_tensor(n_row[:, :], n2[:, :, 0], n2[:, :, 1], ALU.add).then_inc(s("counts"), 1)
                v_.scalar_tensor_tensor(R[:, :, 0:SLOTS], keys1[:, :, :], -CENTRE, some[:, :, :], ALU.add, ALU.mult).then_inc(s("decode"), 1)

            def masks(g):
                base, k = g * STEPS_OF_GROUP, 30
                dve.wait_ge(s("offs"), g + 1)
                v_.tensor_copy(off[:, :], bank[7][:, 0:G]).then_inc(s("decode"), 1)
                v_.scalar_tensor_tensor(end[:, :], bank[7][:, 0:G], -0.5, n_row[:, :], ALU.add, ALU.add).then_inc(s("decode"), 1)
                v_.tensor_copy(R[:, :, SLOTS], bank[7][:, 0:G]).then_inc(s("decode"), 1)
                v_.tensor_tensor(R[:, :, SLOTS + 1], bank[7][:, 0:G], n2[:, :, 0], ALU.add).then_inc(s("R"), 1)
                v_.tensor_scalar(mxt[:, :], bank[7][:, G:2 * G], -float(LISTED), None, ALU.add).then_inc(s("decode"), 1)
                k += 9
                dve.wait_ge(s("decode"), base + k)
                v_.reduce_max(one(bad_all[:, bass.ts(g, 1), 2:3]), mxt[:, :], axis=AX.X).then_inc(s("decode"), 1)
                k += 1
                for t in range(G):
                    v_.tensor_scalar(near[:, t, :], place_row[:, :], off[:, t:t + 1], end[:, t:t + 1], ALU.max, ALU.min).then_inc(s("decode"), 1)
                k += G
                dve.wait_ge(s("decode"), base + k)
                if some_wait(g):
                    dve.wait_ge(s("bias"), 2 * G * g)
                v_.tensor_tensor(mask_list[:, :, :], near[:, :, :], place_row[:, :].unsqueeze(1).broadcast_to([P, G, LISTED]),
                                 ALU.is_equal).then_inc(s("masks"), 1)

            def select(g):
                base, k = g * STEPS_OF_GROUP, 48
                gk = bank[7][:, 0:G * LC * 20].rearrange("p (c e) -> p c e", e=20)
                dve.wait_ge(s("G"), g + 1)
                v_.tensor_tensor(rel[:, :, :], place_col[:, :, :], gk[:, :, SLOTS:SLOTS + 2], ALU.subtract).then_inc(s("decode"), 1)
                k += 1
                dve.wait_ge(s("decode"), base + k)
                v_.tensor_tensor(hit[:, :, :].rearrange("p c (h e) -> p (c h) e", h=2),
                                 rel[:, :, :].rearrange("p c h -> p (c h)").unsqueeze(2).broadcast_to([P, G * LC * 2, 8]),
                                 slot_row[:, :].unsqueeze(1).broadcast_to([P, G * LC * 2, 8]), ALU.is_equal).then_inc(s("decode"), 1)
                k += 1
                dve.wait_ge(s("decode"), base + k)
                v_.tensor_tensor(hitk[:, :, :], hit[:, :, :], gk[:, :, 0:SLOTS], ALU.mult).then_inc(s("decode"), 1)
                k += 1
                dve.wait_ge(s("decode"), base + k)
                v_.reduce_sum(keyf[:, :], hitk[:, :, :], axis=AX.X).then_inc(s("decode"), 1)
                k += 1
                dve.wait_ge(s("decode"), base + k)
                v_.tensor_scalar(keyg[:, :], keyf[:, :], CENTRE - 1.0, 0.0, ALU.add, ALU.max).then_inc(s("decode"), 1)
                k += 1
                dve.wait_ge(s("decode"), base + k)
                v_.tensor_scalar(idx_all[:, bass.ts(g, G), :].rearrange("p t c -> p (t c)"), keyg[:, :], float(N - 1), None, ALU.min).then_inc(s("idx"), 1)
                assert k == STEPS_OF_GROUP

            for i in range(G // 2):
                pack(0, i)
            decode(0)
            compact(0)
            masks(0)
            dve.wait_ge(s("xsum"), 4)
            o = TILES // 2
            v_.tensor_tensor(x_all[:, o:o + 4, :], x_all[:, o:o + 4, :], x_all[:, o + 4:o + 8, :], ALU.add).then_inc(s("xsum_v"), 1)
            dve.wait_ge(s("xsum_v"), 1)
            v_.tensor_tensor(x_all[:, o:o + 2, :], x_all[:, o:o + 2, :], x_all[:, o + 2:o + 4, :], ALU.add).then_inc(s("xsum_v"), 1)
            select(0)

            def scores(t, b, r, Et):
                dve.wait_ge(s("E"), t + 1)
                v_.tensor_tensor(em[b][:, :], Et[:, D:D + 1], Et[:, D + 1:D + 2], ALU.max).then_inc(s("em"), 1)
                dve.wait_ge(s("bias"), 2 * t + 2)
                dve.wait_ge(s("Sp"), t + 1)
                if some_wait(t - 1):
                    dve.wait_ge(s("PTp"), t - 1)
                dve.sem_inc(s("passed_v"), 1)
                v_.tensor_tensor_reduce(out=S[b][:, 0:KEYS], in0=bank[2][:, 0:KEYS], in1=bias[r][:, 0:KEYS], scale=1.0, scalar=-3.0e38,
                                        op0=ALU.add, op1=ALU.max, accum_out=mx[b][:, 0:1]).then_inc(s("Sm"), 1)
                dve.wait_ge(s("Sm"), t + 1)
                dve.wait_ge(s("em"), t + 1)
                v_.tensor_scalar(negm[r][:, :], mx[b][:, :], em[b][:, :], -1.0, ALU.max, ALU.mult).then_inc(s("negm"), 1)

            def epilogue(t, j):
                b, r, q = j % 2, j % AHEAD, j % ROWS
                dve.wait_ge(s("exp"), 2 * t + 2)
                v_.reduce_sum(st[r][:, 3:4], st[r][:, 0:3], axis=AX.X).then_inc(s("ep"), 1)
                v_.tensor_copy(one(negm_all[:, bass.ts(t, 1), :]), negm[r][:, :]).then_inc(s("ep"), 1)
                dve.wait_ge(s("ep"), 3 * t + 1)
                v_.reciprocal(st[r][:, 4:5], st[r][:, 3:4]).then_inc(s("ep"), 1)
                dve.wait_ge(s("parts"), 2 * t + 2)
                dve.wait_ge(s("Wp"), t + 1)
                v_.tensor_tensor(acc[b][:, :], parts[b][0], bank[5][:, 0:D], ALU.add).then_inc(s("acc"), 1)
                dve.wait_ge(s("acc"), t + 1)
                dve.wait_ge(s("ep"), 3 * t + 3)
                dve.wait_ge(s(f"m{q}"), loaded("m", t, q, ROWS))
                dve.wait_ge(s(f"own{q}"), loaded("own", t, q, ROWS, 2))
                v_.scalar_tensor_tensor(acc2[b][:, :], acc[b][:, :], st[r][:, 4:5], m_row[q], ALU.mult, ALU.max).then_inc(s("y"), 1)
                dve.wait_ge(s("y"), 2 * t + 1)
                v_.tensor_tensor(y[b][:, :], acc2[b][:, :], x_own[q], ALU.add).then_inc(s("y"), 1)
                if tile(t - 1):
                    normalise(t - 1, (j + 1) % 2)
                dve.wait_ge(s("y"), 2 * t + 2)
                dve.sem_inc(s("passed_v"), 1)
                v_.bn_stats(stats[b][:, :], y[b][:, :]).then_inc(s("st"), 1)
                dve.wait_ge(s("st"), 2 * t + 1)
                dve.sem_inc(s("passed_v"), 1)
                v_.bn_aggr(mv[b][:, :], stats[b][:, :]).then_inc(s("st"), 1)

            def normalise(t, b):
                dve.wait_ge(s("pw"), 2 * t + 2)
                if some_wait(t - 1):
                    dve.wait_ge(s(f"out{b}"), 8 * (t - b))
                v_.tensor_scalar(o_t[b][:, :], y[b][:, :], mv[b][:, 0:1], rstd[b][:, :], ALU.subtract, ALU.mult).then_inc(s("norm"), 1)

            def step(g, t, j, k):
                if tile(t + 1):
                    scores(t + 1, (k + 1) % 2, (k + 1) % AHEAD, E_of(t + 1, k + 1))
                if tile(t - 1):
                    epilogue(t - 1, (k + 7) % ROWS)
                elif isinstance(t, int) and t == TILES + 1:
                    normalise(TILES - 1, (TILES - 1) % 2)
                if j == 0 and some_wait(g):
                    select(g)
                if listed(g + 1):
                    if 1 <= j <= G // 2:
                        pack(g + 1, j - 1)
                    elif j == G - 3:
                        decode(g + 1)
                    elif j == G - 2:
                        compact(g + 1)
                    elif j == G - 1:
                        masks(g + 1)

            schedule(dve, step)
            v_.reduce_max(verdict[:, 0:1], bad_all[:, :, :].rearrange("p g e -> p (g e)"), axis=AX.X).then_inc(s("verdict"), 1)
            dve.wait_ge(s("ep"), 3 * TILES)
            v_.reduce_max(verdict[:, 1:2], negm_all[:, :, 0], axis=AX.X).then_inc(s("verdict"), 1)
            dve.wait_ge(s("verdict"), 2)
            v_.tensor_scalar(verdict[:, 2:3], verdict[:, 1:2], -SURE, verdict[:, 0:1], ALU.add, ALU.max).then_inc(s("verdict"), 1)
            dve.wait_ge(s("verdict"), 3)
            v_.tensor_scalar(verdict[:, 3:4], verdict[:, 2:3], 0.0, None, ALU.is_gt).then_inc(s("verdict"), 1)
            dve.wait_ge(s("verdictp"), 1)
            v_.tensor_copy(general_i[:, :], bank[7][:, 0:1]).then_inc(s("verdict"), 1)

        @block.tensor
        def _(pe):
            t_ = nc.tensor
            pe.wait_ge(s("const"), 8)
            pe.wait_ge(s("w1"), 48)
            for i, k in enumerate(("wlq", "wlk", "wgq")):
                for d in range(H):
                    for c in range(H):
                        last = t_.transpose(bank[5 + i][:, c * D + d * P:c * D + (d + 1) * P],
                                            w[k][:, d, c * P:(c + 1) * P], ident[:, :])
                last.then_inc(s("wT"), 1)
            pe.wait_ge(s("wTc"), 2)
            for d in range(H):
                for c in range(H):
                    last = t_.matmul(bank[3][:, d * D:(d + 1) * D], wT["wlq"][:, c, d * P:(d + 1) * P],
                                     wT["wlk"][:, c, :], start=(c == 0), stop=(c == H - 1))
            last.then_inc(s("prod"), 1)
            pe.wait_ge(s("prodc"), 1)

            def starts(g):
                pe.wait_ge(s("counts"), g + 1)
                t_.matmul(bank[7][:, 0:G], before[:, :], n_row[:, :], start=True, stop=True)
                t_.matmul(bank[7][:, G:2 * G], ones[:, :], n_row[:, :], start=True, stop=True).then_inc(s("offs"), 1)

            def slots(g):
                pe.wait_ge(s("R"), g + 1)
                pe.wait_ge(s("masks"), g + 1)
                for t in range(G):
                    for c in range(LC):
                        o = (t * LC + c) * 20
                        last = t_.matmul(bank[7][0:FILL[c], o:o + SLOTS + 2],
                                         mask_list[:, t, c * P:c * P + FILL[c]],
                                         R[:, t, :], start=True, stop=True)
                last.then_inc(s("G"), 1)

            def masked_transposed(t, q):
                pe.wait_ge(s(f"m{q}"), loaded("m", t, q, ROWS))
                if some_wait(t):
                    pe.wait_ge(s("TT" if early(t) else "E"), t)
                for h in range(H):
                    ins = t_.transpose(bank[6][:, h * P:(h + 1) * P], m_row[q][:, h * P:(h + 1) * P], ident[:, :])
                ins.then_inc(s("mTp"), 1)

            def masked_keys(t, mT=mT):
                pe.wait_ge(s("mT"), t + 1)
                for o in range(H):
                    for h in range(H):
                        ins = t_.matmul(bank[6][:, o * P:(o + 1) * P], A[:, h, o * P:(o + 1) * P], mT[:, h, :],
                                        start=(h == 0), stop=(h == H - 1))
                ins.then_inc(s("TTp"), 1)

            def masked_values(t, mT=mT):
                if early(t) and t:
                    pe.wait_ge(s("E"), t)
                else:
                    pe.wait_ge(s("TT"), EARLY if early(t) else t + 1)
                for h in range(H):
                    ins = t_.matmul(bank[6][:, 0:D + 2], mT[:, h, :], wevx[:, h, :], start=(h == 0), stop=(h == H - 1))
                ins.then_inc(s("Ep"), 1)

            for t in range(EARLY):
                masked_transposed(t, t)
                masked_keys(t, mT_early[t])
            starts(0)
            for i, n in enumerate((4, 4, 2)):
                if i < 2:
                    pe.wait_ge(s("xsum"), i + 1)
                else:
                    slots(0)
                    pe.wait_ge(s("xsum_v"), 2)
                o = (0, 4, TILES // 2)[i]
                for t in range(o, o + n):
                    for h in range(H):
                        last = t_.matmul(bank[1 + h][:, 0:1], x_all[:, t, h * P:(h + 1) * P], mean_col[:, :],
                                         start=(t == 0), stop=(t == TILES // 2 + 1))
            last.then_inc(s("prod"), 1)
            pe.wait_ge(s("w"), nW)
            pe.wait_ge(s("prodc"), 3)
            for c in range(H):
                for h in range(H):
                    last = t_.matmul(bank[3][:, c:c + 1], w["wgk"][:, h, c * P:(c + 1) * P], xbarB[:, h, 0:1],
                                     start=(h == 0), stop=(h == H - 1))
            last.then_inc(s("prod"), 1)
            pe.wait_ge(s("prodc"), 4)
            for h in range(H):
                for c in range(H):
                    last = t_.matmul(bank[4][:, h:h + 1], wT["wgq"][:, c, h * P:(h + 1) * P], gKT[:, c:c + 1],
                                     start=(c == 0), stop=(c == H - 1))
            last.then_inc(s("prod"), 1)
            pe.wait_ge(s("prodc"), 5)
            masked_values(0, mT_early[0])
            for h in range(H):
                t_.matmul(bank[0][:, 0:D], xbarB[:, h, :], w["wgv"][:, h, :], start=(h == 0), stop=False)
            t_.matmul(bank[0][:, 0:D], ones[0:1, :], bgv_b[0:1, :], start=False, stop=True).then_inc(s("prod"), 1)
            pe.wait_ge(s("prodc"), 6)

            def step(g, t, j, k):
                if tile(t):
                    b = k % 2
                    pe.wait_ge(s("exp"), 2 * t + 1)
                    if some_wait(t):
                        pe.wait_ge(s("PT"), t)
                    for c, n in enumerate([P] + FILL):
                        ins = t_.transpose(bank[3][0:n, c * P:(c + 1) * P], S[b][:, c * P:c * P + n], ident[:, :])
                    ins.then_inc(s("PTp"), 1)
                if tile(t + 1):
                    b = (k + 1) % 2
                    pe.wait_ge(s("TT"), t + 2)
                    pe.wait_ge(s("xT"), 2 * t + 4)
                    if some_wait(t + 1):
                        pe.wait_ge(s("Sm"), t + 1)
                    for h in range(H):
                        ins = t_.matmul(bank[2][:, 0:KEYS], TT_of(t + 1, k + 1)[:, h * P:(h + 1) * P], xT[b][:, h, 0:KEYS], start=(h == 0), stop=(h == H - 1))
                    ins.then_inc(s("Sp"), 1)
                if tile(t - 1):
                    pe.wait_ge(s("OT"), t)
                    if some_wait(t - 1):
                        pe.wait_ge(s("acc"), t - 1)
                    for h in range(H):
                        ins = t_.matmul(bank[5][:, 0:D], OT[(k + 1) % 2][:, h, :], w["wlv"][:, h, :], start=(h == 0), stop=(h == H - 1))
                    ins.then_inc(s("Wp"), 1)
                if tile(t + 2):
                    q, r = (k + 2) % ROWS, (k + 2) % AHEAD
                    if not early(t + 2):
                        masked_transposed(t + 2, q)
                    pe.wait_ge(s(f"own{q}"), loaded("own", t + 2, q, ROWS, 2))
                    pe.wait_ge(s(f"gath{r}"), loaded("gath", t + 2, r, AHEAD, LC))
                    for h in range(H):
                        if some_wait(t + 2):
                            pe.wait_ge(s("xT"), 2 * t + h + 3)
                        t_.transpose(bank[h][:, 0:P], x_own[q][:, h * P:(h + 1) * P], ident[:, :])
                        for c in range(LC):
                            n = FILL[c]
                            ins = t_.transpose(bank[h][:, (c + 1) * P:(c + 1) * P + n], x_list[r][0:n, c, h * P:(h + 1) * P], ident[0:n, 0:n])
                        ins.then_inc(s("xTp"), 1)
                    if not early(t + 2):
                        masked_keys(t + 2)
                if j == G - 1 and listed(g + 1):
                    starts(g + 1)
                elif j == 0 and some_wait(g):
                    slots(g)
                if tile(t):
                    q, r, b = k, k % AHEAD, k % 2
                    pe.wait_ge(s("PT"), t + 1)
                    if some_wait(t):
                        pe.wait_ge(s("OT"), t)
                    for h in range(H):
                        t_.matmul(bank[4][:, h * P:(h + 1) * P], x_own[q][:, h * P:(h + 1) * P], PT[b][:, 0, :], start=True, stop=False)
                        for c in range(LC):
                            ins = t_.matmul(bank[4][:, h * P:(h + 1) * P], x_list[r][0:FILL[c], c, h * P:(h + 1) * P], PT[b][0:FILL[c], c + 1, :],
                                            start=False, stop=(c == LC - 1))
                    ins.then_inc(s("OTp"), 1)
                for v in values_of(t):
                    masked_values(v, mT_early[v] if early(v) else mT)

            schedule(pe, step)
            pe.wait_ge(s("verdict"), 4)
            t_.matmul(bank[7][:, 0:1], ones[:, :], verdict[:, 3:4], start=True, stop=True).then_inc(s("verdictp"), 1)

        block_ctx.__exit__(None, None, None)

        xT_all = area[:, :, :]
        adj_g = adj_p[0][:, 0, :]
        Eg = or1[:, :, :].rearrange("p j n -> p (j n)").bitcast(F32)[:, 0:D + 2]
        Og = adj_p[0][:, 1, 0:4 * D].bitcast(F32)
        m_g, mT_g, TT_g, PT_g, OT_g, st_g = S[0][:, 0:D], mT, TT[0], PT, OT[0], st[0]
        acc_g, acc2_g, y_g, o_g, mv_g, rstd_g, ve_g, stats_g = acc[0], acc2[0], y[0], o_t[0], mv[0], rstd[0], ve[0], stats[0]
        for n in ("x adj m fill mTp mT TTp TT Ep E S Sm nmax exp PTp PT PV Ox OTp OT O y pw norm out xtp xtc chain".split()):
            s("g_" + n)

        gblock = ctx.enter_context(nc.Block())

        @gblock.sync
        def _(sp):
            general = sp.value_load(general_i[0:1, 0:1], min_val=0, max_val=P)
            with sp.If(general != 0):
                for q in range(4):
                    ts = slice(q * TILES // 4, (q + 1) * TILES // 4)
                    sp.dma_start(x_all[:, ts, :], rows(x)[:, ts, :]).then_inc(s("g_x"), 16)
                sp.dma_start(adj_g, adj[0:P, :]).then_inc(s("g_adj"), 16)
                sp.dma_start(m_g, masked_x[0:P, :]).then_inc(s("g_m"), 16)
                with sp.Fori(1, TILES) as t:
                    sp.wait_ge(s("g_Sm"), t * GROUPS)
                    sp.dma_start(adj_g, adj[bass.ts(t, P), :]).then_inc(s("g_adj"), 16)
                    sp.wait_ge(s("g_norm"), t)
                    sp.dma_start(out[bass.ts(t - 1, P), :], o_g[:, :]).then_inc(s("g_out"), 16)
                    sp.wait_ge(s("g_out"), 16 * t)
                    sp.dma_start(m_g, masked_x[bass.ts(t, P), :]).then_inc(s("g_m"), 16)
                sp.wait_ge(s("g_norm"), TILES)
                sp.dma_start(out[(TILES - 1) * P:N, :], o_g[:, :]).then_inc(s("g_out"), 16)
                sp.wait_ge(s("g_out"), 16 * TILES)

        @gblock.gpsimd
        def _(pool):
            g_ = nc.gpsimd
            general = pool.value_load(general_i[0:1, 0:1], min_val=0, max_val=P)
            with pool.If(general != 0):
                g_.memset(Sg[:, :], MASKED).then_inc(s("g_fill"), 1)
                with pool.Fori(0, TILES) as t:
                    pool.wait_ge(s("g_y"), 4 * t + 4)
                    g_.tensor_tensor(ve_g[:, :], mv_g[:, 1:2], eps_col[:, :], ALU.add).then_inc(s("g_pw"), 1)
                    pool.wait_ge(s("g_pw"), 2 * t + 1)
                    g_.tensor_tensor(rstd_g[:, :], ve_g[:, :], power[:, :], ALU.pow).then_inc(s("g_pw"), 1)
                    pool.wait_ge(s("g_PTp"), t * GROUPS + GROUPS)
                    pool.sem_inc(s("passed_p"), 1)
                    g_.memset(Sg[:, :], MASKED).then_inc(s("g_fill"), 1)

        @gblock.scalar
        def _(act):
            a_ = nc.scalar
            general = act.value_load(general_i[0:1, 0:1], min_val=0, max_val=P)
            with act.If(general != 0):
                with act.Fori(0, TILES // 2) as c:
                    act.wait_ge(s("g_xtp"), c + 1)
                    a_.copy(xT_all[:, :, bass.ts(c, 2 * P)], halves(bank[6][:, :])).then_inc(s("g_xtc"), 1)
                with act.Fori(0, TILES) as t:
                    act.wait_ge(s("g_mTp"), t + 1)
                    a_.copy(mT_g[:, :, :], halves(bank[0][:, 0:D])).then_inc(s("g_mT"), 1)
                    act.wait_ge(s("g_TTp"), t + 1)
                    a_.copy(TT_g[:, :], bank[1][:, 0:D]).then_inc(s("g_TT"), 1)
                    act.wait_ge(s("g_nmax"), t + 1)
                    a_.activation(Sg[:, :], Sg[:, :], ACT.Exp, bias=st_g[:, 6:7], accum_out=st_g[:, 0:1]).then_inc(s("g_exp"), 1)
                    a_.activation(st_g[:, 1:3], Eg[:, D:D + 2], ACT.Exp, bias=st_g[:, 6:7]).then_inc(s("g_exp"), 1)
                    for g in range(1, GROUPS, 2):
                        act.wait_ge(s("g_PTp"), t * GROUPS + g + 1)
                        a_.copy(PT_g[1][:, :, :], bank[2 + g % 2][:, :].rearrange("p (c q) -> p c q", c=CHUNKS)).then_inc(s("g_PT"), 1)
                    act.wait_ge(s("g_OTp"), t + 1)
                    a_.copy(OT_g[:, :, :], halves(bank[0][:, 0:D])).then_inc(s("g_OT"), 1)

        @gblock.vector
        def _(dve):
            v_ = nc.vector
            general = dve.value_load(general_i[0:1, 0:1], min_val=0, max_val=P)
            with dve.If(general != 0):
                with dve.Fori(0, TILES) as t:
                    dve.wait_ge(s("g_Ep"), t + 1)
                    v_.tensor_copy(Eg, bank[7][:, 0:D + 2]).then_inc(s("g_E"), 1)
                    dve.wait_ge(s("g_fill"), t + 1)
                    dve.wait_ge(s("g_adj"), 16 * t + 16)
                    for g in range(GROUPS):
                        dve.wait_ge(s("g_S"), t * GROUPS + g + 1)
                        dve.sem_inc(s("passed_v"), 1)
                        v_.copy_predicated(Sg[:, g * GROUP:(g + 1) * GROUP], adj_g[:, g * GROUP:(g + 1) * GROUP],
                                           bank[4 + g % 2][:, :]).then_inc(s("g_Sm"), 1)
                    dve.wait_ge(s("g_Sm"), (t + 1) * GROUPS)
                    v_.reduce_max(st_g[:, 3:4], Sg[:, :], axis=AX.X).then_inc(s("g_chain"), 1)
                    dve.wait_ge(s("g_E"), t + 1)
                    v_.reduce_max(st_g[:, 5:6], Eg[:, D:D + 2], axis=AX.X).then_inc(s("g_chain"), 1)
                    dve.wait_ge(s("g_chain"), 8 * t + 2)
                    v_.tensor_scalar(st_g[:, 6:7], st_g[:, 3:4], st_g[:, 5:6], -1.0, ALU.max, ALU.mult).then_inc(s("g_nmax"), 1)
                    for g in range(0, GROUPS, 2):
                        dve.wait_ge(s("g_PTp"), t * GROUPS + g + 1)
                        v_.tensor_copy(PT_g[0][:, :, :], bank[2 + g % 2][:, :].rearrange("p (c q) -> p c q", c=CHUNKS)).then_inc(s("g_PT"), 1)
                    dve.wait_ge(s("g_PV"), (t + 1) * GROUPS)
                    v_.tensor_copy(Og, bank[6][:, 0:D]).then_inc(s("g_Ox"), 1)
                    dve.wait_ge(s("g_exp"), 2 * t + 2)
                    v_.reduce_sum(st_g[:, 7:8], st_g[:, 0:3], axis=AX.X).then_inc(s("g_chain"), 1)
                    dve.wait_ge(s("g_chain"), 8 * t + 3)
                    v_.reciprocal(st_g[:, 4:5], st_g[:, 7:8]).then_inc(s("g_chain"), 1)
                    v_.tensor_tensor(acc_g[:, :], Eg[:, 0:D], bev_b[:, 0:D], ALU.add).then_inc(s("g_chain"), 1)
                    dve.wait_ge(s("g_O"), t + 1)
                    dve.wait_ge(s("g_chain"), 8 * t + 5)
                    v_.scalar_tensor_tensor(acc2_g[:, :], acc_g[:, :], st_g[:, 2:3], bank[7][:, 0:D], ALU.mult, ALU.add).then_inc(s("g_chain"), 1)
                    dve.wait_ge(s("g_chain"), 8 * t + 6)
                    v_.scalar_tensor_tensor(acc_g[:, :], gV_b[:, :], st_g[:, 1:2], acc2_g[:, :], ALU.mult, ALU.add).then_inc(s("g_chain"), 1)
                    dve.wait_ge(s("g_chain"), 8 * t + 7)
                    v_.scalar_tensor_tensor(acc2_g[:, :], blv_b[:, :], st_g[:, 0:1], acc_g[:, :], ALU.mult, ALU.add).then_inc(s("g_chain"), 1)
                    dve.wait_ge(s("g_chain"), 8 * t + 8)
                    dve.wait_ge(s("g_m"), 16 * t + 16)
                    v_.scalar_tensor_tensor(acc_g[:, :], acc2_g[:, :], st_g[:, 4:5], m_g, ALU.mult, ALU.max).then_inc(s("g_y"), 1)
                    dve.wait_ge(s("g_y"), 4 * t + 1)
                    v_.tensor_tensor(y_g[:, :], acc_g[:, :], one(x_all[:, bass.ts(t, 1), :]), ALU.add).then_inc(s("g_y"), 1)
                    dve.wait_ge(s("g_y"), 4 * t + 2)
                    dve.sem_inc(s("passed_v"), 1)
                    v_.bn_stats(stats_g[:, :], y_g[:, :]).then_inc(s("g_y"), 1)
                    dve.wait_ge(s("g_y"), 4 * t + 3)
                    dve.sem_inc(s("passed_v"), 1)
                    v_.bn_aggr(mv_g[:, :], stats_g[:, :]).then_inc(s("g_y"), 1)
                    dve.wait_ge(s("g_pw"), 2 * t + 2)
                    v_.tensor_scalar(o_g[:, :], y_g[:, :], mv_g[:, 0:1], rstd_g[:, :], ALU.subtract, ALU.mult).then_inc(s("g_norm"), 1)

        @gblock.tensor
        def _(pe):
            t_ = nc.tensor
            general = pe.value_load(general_i[0:1, 0:1], min_val=0, max_val=P)
            with pe.If(general != 0):
                pe.wait_ge(s("g_x"), 64)
                for c in range(TILES // 2):
                    if c >= 1:
                        pe.wait_ge(s("g_xtc"), c)
                    for j in range(2):
                        for h in range(H):
                            last = t_.transpose(bank[6][:, h * 2 * P + j * P:h * 2 * P + (j + 1) * P],
                                                x_all[:, 2 * c + j, h * P:(h + 1) * P], ident[:, :])
                    last.then_inc(s("g_xtp"), 1)
                pe.wait_ge(s("g_xtc"), TILES // 2)
                with pe.Fori(0, TILES) as t:
                    pe.wait_ge(s("g_m"), 16 * t + 16)
                    for h in range(H):
                        last = t_.transpose(bank[0][:, h * P:(h + 1) * P], m_g[:, h * P:(h + 1) * P], ident[:, :])
                    last.then_inc(s("g_mTp"), 1)
                    pe.wait_ge(s("g_mT"), t + 1)
                    for o in range(H):
                        for h in range(H):
                            last = t_.matmul(bank[1][:, o * P:(o + 1) * P], A[:, h, o * P:(o + 1) * P], mT_g[:, h, :],
                                             start=(h == 0), stop=(h == H - 1))
                    last.then_inc(s("g_TTp"), 1)
                    for h in range(H):
                        last = t_.matmul(bank[7][:, 0:D + 2], mT_g[:, h, :], wevx[:, h, :], start=(h == 0), stop=(h == H - 1))
                    last.then_inc(s("g_Ep"), 1)
                    pe.wait_ge(s("g_TT"), t + 1)
                    for g in range(GROUPS):
                        if g >= 2:
                            pe.wait_ge(s("g_Sm"), t * GROUPS + g - 1)
                        for h in range(H):
                            last = t_.matmul(bank[4 + g % 2][:, :], TT_g[:, h * P:(h + 1) * P], xT_all[:, h, g * GROUP:(g + 1) * GROUP],
                                             start=(h == 0), stop=(h == H - 1))
                        last.then_inc(s("g_S"), 1)

                    def transposes(g):
                        if g >= 2:
                            pe.wait_ge(s("g_PT"), t * GROUPS + g - 1)
                        for c in range(CHUNKS):
                            k = g * GROUP + c * P
                            last = t_.transpose(bank[2 + g % 2][:, c * P:(c + 1) * P], Sg[:, k:k + P], ident[:, :])
                        last.then_inc(s("g_PTp"), 1)

                    def products(g):
                        pe.wait_ge(s("g_PT"), t * GROUPS + g + 1)
                        for c in range(CHUNKS):
                            last = t_.matmul(bank[6][:, 0:D], PT_g[g % 2][:, c, :], x_all[:, g * CHUNKS + c, 0:D],
                                             start=(g == 0 and c == 0), stop=(g == GROUPS - 1 and c == CHUNKS - 1))
                        last.then_inc(s("g_PV"), 1)

                    pe.wait_ge(s("g_exp"), 2 * t + 1)
                    transposes(0)
                    for g in range(GROUPS):
                        products(g)
                        if g + 1 < GROUPS:
                            transposes(g + 1)
                    pe.wait_ge(s("g_Ox"), t + 1)
                    for h in range(H):
                        last = t_.transpose(bank[0][:, h * P:(h + 1) * P], Og[:, h * P:(h + 1) * P], ident[:, :])
                    last.then_inc(s("g_OTp"), 1)
                    pe.wait_ge(s("g_OT"), t + 1)
                    for h in range(H):
                        last = t_.matmul(bank[7][:, 0:D], OT_g[:, h, :], w["wlv"][:, h, :], start=(h == 0), stop=(h == H - 1))
                    last.then_inc(s("g_O"), 1)


_INS = ["x", "adj", "L0_gnn_masked_x", "L0_gnn_Wlq", "L0_gnn_Wlk", "L0_gnn_Wlv", "L0_gnn_blv", "L0_gnn_Wgq",
        "L0_gnn_Wgk", "L0_gnn_Wgv", "L0_gnn_bgv", "L0_gnn_Wes", "L0_gnn_Wev", "L0_gnn_bev"]


def kernel(**inputs):
    import concourse.bacc as bacc
    from concourse.bass_utils import run_bass_kernel_spmd

    nc = bacc.Bacc("TRN2", target_bir_lowering=False, num_devices=1)
    arrays, args = {}, []
    for name in _INS:
        a = np.ascontiguousarray(inputs[name])
        arrays[f"in_{name}"] = a
        args.append(nc.dram_tensor(f"in_{name}", a.shape, mybir.dt.from_np(a.dtype), kind="ExternalInput").ap())
    args.append(nc.dram_tensor("out_rows", (N, D), F32, kind="ExternalOutput").ap())
    build(nc, *args)
    r = run_bass_kernel_spmd(nc, [arrays], core_ids=[0])
    return r.results[0]["out_rows"]
```
